# Optimizing a Trainium2 kernel written in Bass

```python
import numpy as np
import jax
import jax.numpy as jnp

def _softmax(x, axis=-1):
    return jax.nn.softmax(x, axis=axis)

def _gelu(x):
    return jax.nn.gelu(x, approximate=True)

def _silu(x):
    return jax.nn.silu(x)

def _sigmoid(x):
    return jax.nn.sigmoid(x)

def _layernorm(x, axis=-1, eps=1e-05):
    m = jnp.mean(x, axis=axis, keepdims=True)
    v = jnp.var(x, axis=axis, keepdims=True)
    return (x - m) / jnp.sqrt(v + eps)

def _scatter_add(tgt, idx, src, axis=0):
    return tgt.at[idx].add(src)

def _segment_sum(src, seg, n):
    return jax.ops.segment_sum(src, seg, n)
kernel_name = 'mk_adj_ffn_d1_adj_r2_b69c95'

def setup_inputs(seed: int=0):
    np.random.seed(seed)
    _w = jnp.asarray

    def _rec_inputs():
        import jax
        import jax.numpy as jnp
        _gk = jax.random.key(seed)
        x = -7.109e-05 + 0.9999 * jax.random.normal(jax.random.fold_in(_gk, 1), (128, 64, 256), jnp.float32)
        _w = (1.0 + jnp.arange(64, dtype=jnp.float32)) ** (-0.5)
        _w = _w / _w.mean()
        _pij = jnp.clip(0.0625 * _w[:, None] * _w[None, :], 0.0, 1.0)
        _a = jax.random.uniform(jax.random.fold_in(_gk, 2), (128, 64, 64)) < _pij
        adj = _a
        return (x, adj)
    x, adj = _rec_inputs()

    def _L0_gnn_setup():
        import jax, jax.numpy as jnp
        import numpy as np
        B, S, D, H = (1024, 64, 256, 8)
        HD = D // H
        SCALE = float(1.0 / np.sqrt(HD))

        def _static_masks():
            sq = np.arange(64)
            r = sq // 8
            f = sq % 8
            ri, rj = (r[:, None], r[None, :])
            fi, fj = (f[:, None], f[None, :])
            dr = np.abs(ri - rj)
            df = np.abs(fi - fj)
            eye = np.eye(64, dtype=bool)
            file_m = fi == fj
            rank_m = ri == rj
            diag_m = ri - fi == rj - fj
            adiag_m = ri + fi == rj + fj
            knight_m = (dr == 2) & (df == 1) | (dr == 1) & (df == 2) | eye
            king_m = (dr <= 1) & (df <= 1)
            return np.stack([file_m, rank_m, diag_m, adiag_m, knight_m, king_m])
        STATIC = jnp.asarray(_static_masks())
        EYE = jnp.eye(S, dtype=bool)
        key = jax.random.key(seed)
        ks = jax.random.split(key, 7)
        x = jax.random.normal(ks[0], (B, S, D), jnp.float32)
        ray_mask = jax.random.bernoulli(ks[1], 0.15, (B, S, S))
        attack_mask = jax.random.bernoulli(ks[2], 0.1, (B, S, S))
        s = 1.0 / np.sqrt(D)

        def lin(k):
            k1, k2 = jax.random.split(k)
            W = jax.random.uniform(k1, (D, D), jnp.float32, -s, s)
            b = jax.random.uniform(k2, (D,), jnp.float32, -s, s)
            return (W, b)
        Wq, bq = lin(ks[3])
        Wk, bk = lin(ks[4])
        Wv, bv = lin(ks[5])
        Wo, bo = lin(ks[6])
        return dict(x=x, ray_mask=ray_mask, attack_mask=attack_mask, Wq=Wq, bq=bq, Wk=Wk, bk=bk, Wv=Wv, bv=bv, Wo=Wo, bo=bo)
    _L0_gnn_all = _L0_gnn_setup()
    _L0_gnn_in = {k: v for k, v in _L0_gnn_all.items() if k in ('Wq', 'bq', 'Wk', 'bk', 'Wv', 'bv', 'Wo', 'bo')}
    del _L0_gnn_all

    def _L0_ffn_setup():
        import jax, jax.numpy as jnp
        import numpy as np
        TOP_K = 2
        key = jax.random.key(seed)
        k1, k2, k3, k4 = jax.random.split(key, 4)
        B, S, d = (4, 1024, 256)
        E, H = (32, 128)
        x = jax.random.normal(k1, (B, S, d), dtype=jnp.float32)
        expert_sel = jax.random.normal(k2, (E, d), dtype=jnp.float32) / np.sqrt(d).astype(np.float32)
        keys = jax.random.normal(k3, (E, d, H), dtype=jnp.float32) / np.sqrt(d).astype(np.float32)
        values = jax.random.normal(k4, (E, H, d), dtype=jnp.float32) / np.sqrt(E * H).astype(np.float32)
        return {'x': x, 'expert_sel': expert_sel, 'keys': keys, 'values': values}
    _L0_ffn_all = _L0_ffn_setup()
    _L0_ffn_in = {k: v for k, v in _L0_ffn_all.items() if k in ('expert_sel', 'keys', 'values')}
    del _L0_ffn_all
    return {'x': x, 'adj': adj, 'L0_gnn_Wq': _L0_gnn_in['Wq'], 'L0_gnn_bq': _L0_gnn_in['bq'], 'L0_gnn_Wk': _L0_gnn_in['Wk'], 'L0_gnn_bk': _L0_gnn_in['bk'], 'L0_gnn_Wv': _L0_gnn_in['Wv'], 'L0_gnn_bv': _L0_gnn_in['bv'], 'L0_gnn_Wo': _L0_gnn_in['Wo'], 'L0_gnn_bo': _L0_gnn_in['bo'], 'L0_ffn_expert_sel': _L0_ffn_in['expert_sel'], 'L0_ffn_keys': _L0_ffn_in['keys'], 'L0_ffn_values': _L0_ffn_in['values']}

def reference(x, adj, L0_gnn_Wq, L0_gnn_bq, L0_gnn_Wk, L0_gnn_bk, L0_gnn_Wv, L0_gnn_bv, L0_gnn_Wo, L0_gnn_bo, L0_ffn_expert_sel, L0_ffn_keys, L0_ffn_values):
    import jax
    import jax.numpy as jnp

    def _L0_gnn_ref(x, ray_mask, attack_mask, Wq, bq, Wk, bk, Wv, bv, Wo, bo):
        import jax, jax.numpy as jnp
        import numpy as np
        B, S, D, H = (1024, 64, 256, 8)
        HD = D // H
        SCALE = float(1.0 / np.sqrt(HD))

        def _static_masks():
            sq = np.arange(64)
            r = sq // 8
            f = sq % 8
            ri, rj = (r[:, None], r[None, :])
            fi, fj = (f[:, None], f[None, :])
            dr = np.abs(ri - rj)
            df = np.abs(fi - fj)
            eye = np.eye(64, dtype=bool)
            file_m = fi == fj
            rank_m = ri == rj
            diag_m = ri - fi == rj - fj
            adiag_m = ri + fi == rj + fj
            knight_m = (dr == 2) & (df == 1) | (dr == 1) & (df == 2) | eye
            king_m = (dr <= 1) & (df <= 1)
            return np.stack([file_m, rank_m, diag_m, adiag_m, knight_m, king_m])
        STATIC = jnp.asarray(_static_masks())
        EYE = jnp.eye(S, dtype=bool)
        Bn = x.shape[0]

        def split_heads(t):
            return t.reshape(Bn, S, H, HD).transpose(0, 2, 1, 3)
        q = split_heads(x @ Wq.T + bq)
        k = split_heads(x @ Wk.T + bk)
        v = split_heads(x @ Wv.T + bv)
        scores = jnp.einsum('bhsd,bhtd->bhst', q, k) * SCALE
        mask = jnp.concatenate([jnp.broadcast_to(STATIC[None], (Bn, 6, S, S)), (ray_mask | EYE)[:, None], (attack_mask | EYE)[:, None]], axis=1)
        scores = jnp.where(mask, scores, jnp.float32(-1000000000.0))
        attn = jax.nn.softmax(scores, axis=-1)
        out = jnp.einsum('bhst,bhtd->bhsd', attn, v)
        out = out.transpose(0, 2, 1, 3).reshape(Bn, S, D)
        return out @ Wo.T + bo

    def _L0_ffn_ref(x, expert_sel, keys, values):
        import jax, jax.numpy as jnp
        import numpy as np
        TOP_K = 2
        B, S, d = x.shape
        E = keys.shape[0]
        xt = x.reshape(-1, d)
        T = xt.shape[0]
        sel = jax.nn.sigmoid(xt @ expert_sel.T)
        sel_val, sel_idx = jax.lax.top_k(sel, TOP_K)
        w = jnp.zeros((T, E), dtype=xt.dtype).at[jnp.arange(T)[:, None], sel_idx].add(sel_val)
        h = jax.nn.relu(jnp.einsum('td,edh->teh', xt, keys))
        out = jnp.einsum('teh,te,ehv->tv', h, w, values)
        return out.reshape(B, S, -1)
    x = x + _L0_gnn_ref(_layernorm(x, axis=-1), adj, adj, L0_gnn_Wq, L0_gnn_bq, L0_gnn_Wk, L0_gnn_bk, L0_gnn_Wv, L0_gnn_bv, L0_gnn_Wo, L0_gnn_bo)
    x = x + _L0_ffn_ref(_layernorm(x, axis=-1), L0_ffn_expert_sel, L0_ffn_keys, L0_ffn_values)
    return x

_drawn_inputs = setup_inputs


def setup_inputs(seed=0):
    import zlib

    import numpy as np

    out = dict(_drawn_inputs(seed))
    spreads = {}
    factors = {'L0_gnn_bq': 6.414, 'L0_gnn_bk': 8.0}
    for name, (base, spread) in spreads.items():
        noise = np.random.default_rng([zlib.crc32(name.encode()), seed]).standard_normal(out[name].shape)
        drawn = base * np.exp(spread * noise) if base else spread * noise
        out[name] = jnp.asarray(drawn.astype(out[name].dtype))
    for name, factor in factors.items():
        out[name] = (out[name] * factor).astype(out[name].dtype)
    return out
```

```python
from contextlib import ExitStack

import concourse.bass as bass
from concourse import mybir

F32 = mybir.dt.float32
F32R = mybir.dt.float32r
BF16 = mybir.dt.bfloat16
I32 = mybir.dt.int32
U32 = mybir.dt.uint32
U8 = mybir.dt.uint8
ALU = mybir.AluOpType
ACT = mybir.ActivationFunctionType
AX = mybir.AxisListType

P = 128
BOARDS, SQ, D = 128, 64, 256
HEADS = 8
HD = D // HEADS
EXPERTS, HID = 32, 128
TOKENS = BOARDS * SQ
TILES = TOKENS // P
UNITS = TILES // 2
FC = D // P
SCALE = HD ** -0.5
EPS = 1e-5
MASKED = -1e9
BLOCKS = 2 * TOKENS // P + EXPERTS
ROWS = BLOCKS * P
QPAD = 4 * P


def static_masks():
    import numpy as np
    sq = np.arange(SQ)
    r, f = sq // 8, sq % 8
    ri, rj, fi, fj = r[:, None], r[None, :], f[:, None], f[None, :]
    dr, df = np.abs(ri - rj), np.abs(fi - fj)
    eye = np.eye(SQ, dtype=bool)
    masks = [fi == fj, ri == rj, ri - fi == rj - fj, ri + fi == rj + fj,
             ((dr == 2) & (df == 1)) | ((dr == 1) & (df == 2)) | eye, (dr <= 1) & (df <= 1)]
    bias = np.where(np.stack(masks, 1), 0.0, MASKED)
    return np.concatenate([bias, bias]).astype(np.float32)


def constants():
    import numpy as np
    eye = np.eye(P, dtype=np.float32)
    return {
        "c_static": static_masks(),
        "c_eye": eye,
        "c_others": np.concatenate([np.where(np.eye(SQ), 0, MASKED).astype(np.float32)] * 2),
        "c_before": np.triu(np.ones((P, P), np.float32), 1),
        "c_iota": np.tile(np.arange(EXPERTS, dtype=np.float32), (P, 1)),
    }


def build(nc, x, adj, wqkv, wo, bqkv, bo, sel, keys, values, c_static, c_eye, c_others,
          c_before, c_iota, out):
    ctx = ExitStack()
    with ctx:
        def sb(name, shape, dt, where=ctx):
            return where.enter_context(nc.sbuf_tensor(name, shape, dt))

        def sem(name):
            return ctx.enter_context(nc.semaphore(name))

        rows_in = nc.dram_tensor("rows_in", (ROWS, D), F32).ap()
        rows_out = nc.dram_tensor("rows_out", (ROWS, D), F32).ap()
        block_row = nc.dram_tensor("block_row", (P * 2,), I32).ap()

        x_all = sb("x_all", [P, TILES, D], F32)
        keys_sb = sb("keys_sb", [P, EXPERTS, FC, HID], F32)
        adj_sb = sb("adj_sb", [P, TILES, SQ], U8)
        static_sb = sb("static_sb", [P, 6, SQ], BF16)
        eye = sb("eye", [P, P], F32)
        eyeb = sb("eyeb", [P, P], BF16)
        before = sb("before", [P, P], BF16)
        onesb = sb("onesb", [P, P], BF16)
        iota = sb("iota", [P, EXPERTS], F32)
        pidx = sb("pidx", [P, 2], I32)
        pidxf = sb("pidxf", [P, 2], F32)
        zeros = sb("zeros", [P, D], F32)
        ln2_all = sb("ln2_all", [P, TILES, 2], F32)
        top_all = sb("top_all", [P, TILES, 2], F32)
        onehot = sb("onehot", [P, TILES, 2, EXPERTS], BF16)
        rank_all = sb("rank_all", [P, TILES, EXPERTS], F32)
        carry = sb("carry", [P, EXPERTS], F32)
        slot = sb("slot", [P, TILES * 2], I32)
        slotf = sb("slotf", [P, TILES * 2], F32)
        cum = sb("cum", [P, 2, EXPERTS], F32)
        blocksi = sb("blocksi", [P, 2, EXPERTS], I32)
        blocksf = sb("blocksf", [P, EXPERTS], F32)
        base = sb("base", [P, EXPERTS], F32)
        below = sb("below", [P, 2, EXPERTS], F32)
        owner = sb("owner", [P, 2], F32)
        owneri = sb("owneri", [P, 2], I32)
        owner_row = sb("owner_row", [1, P * 2], I32)

        early = ExitStack()
        wqkv_h = sb("wqkv_h", [P, FC, 3 * D], F32R, early)
        wqkv_l = sb("wqkv_l", [P, FC, 3 * D], F32R, early)
        wo_h = sb("wo_h", [P, FC, D], F32R, early)
        wo_l = sb("wo_l", [P, FC, D], F32R, early)
        kbd_h = sb("kbd_h", [P, FC, 4, 2 * P], F32R, early)
        kbd_l = sb("kbd_l", [P, FC, 4, 2 * P], F32R, early)
        qz_h = sb("qz_h", [P, FC, QPAD], F32R, early)
        qz_l = sb("qz_l", [P, FC, QPAD], F32R, early)
        k_h = sb("k_h", [P, FC, 2 * P], F32R, early)
        k_l = sb("k_l", [P, FC, 2 * P], F32R, early)
        xt_h = sb("xt_h", [P, FC, 2 * P], F32R, early)
        xt_l = sb("xt_l", [P, FC, 2 * P], F32R, early)
        vbd = sb("vbd", [P, 2, 2, 4, 2, HD], F32, early)
        probs = sb("probs", [P, 2, 512], F32, early)
        probs_t = sb("probs_t", [P, 2, 512], F32, early)
        ot_h = sb("ot_h", [P, 2, FC, P], F32R, early)
        ot_l = sb("ot_l", [P, 2, FC, P], F32R, early)
        xn = sb("xn", [P, 2, D], F32, early)
        xn2 = sb("xn2", [P, 2, D], F32, early)
        x2t = sb("x2t", [P, FC, 2 * P], F32, early)
        sel_sb = sb("sel_sb", [P, FC, EXPERTS], F32, early)
        bias_sb = sb("bias_sb", [P, 3, FC], F32, early)
        bq_s = sb("bq_s", [P, FC], F32, early)
        bo_sb = sb("bo_sb", [P, D], F32, early)
        others = sb("others", [P, SQ], F32, early)
        adj_f = sb("adj_f", [P, 2, SQ], F32, early)
        adj_bias = sb("adj_bias", [P, 2, SQ], BF16, early)
        st1 = sb("st1", [P, 2, 6], F32, early)
        st2 = sb("st2", [P, 2, 6], F32, early)
        mv = sb("mv", [P, 4, 2], F32, early)
        ve = sb("ve", [P, 4], F32, early)
        minus_half = sb("minus_half", [P, 4], F32, early)
        rstd = sb("rstd", [P, 4], F32, early)
        nmax = sb("nmax", [P, 2, HEADS], F32, early)
        psum_p = sb("psum_p", [P, 2, HEADS], F32, early)
        rsum = sb("rsum", [P, 2, HEADS], F32, early)
        egate = sb("egate", [P, 2, EXPERTS], F32, early)
        egate1 = sb("egate1", [P, 2, EXPERTS], F32, early)
        gate = sb("gate", [P, 2, EXPERTS], F32, early)
        top = sb("top", [P, 2, 8], F32, early)
        topi = sb("topi", [P, 2, 8], U32, early)
        topf = sb("topf", [P, 2, 2], F32, early)
        picks = sb("picks", [P, 2, 2, EXPERTS], BF16, early)
        chosen = sb("chosen", [P, 2, EXPERTS], BF16, early)
        early.close()
        values_sb = sb("values_sb", [P, EXPERTS, D], F32)
        spread = sb("spread", [P, TILES, 2, EXPERTS // 2], F32)
        NSC = 4
        xs = sb("xs", [P, NSC, D], F32)
        NX = 4
        xg = sb("xg", [P, NX, D], F32)
        xgt = sb("xgt", [P, 2, FC, P], F32)
        hid = sb("hid", [P, 2, HID], F32)
        hidt = sb("hidt", [P, 2, P], F32)
        yb = sb("yb", [P, 2, D], F32)
        NG = 4
        ga = sb("ga", [P, NG, 2, D], F32)
        yo = sb("yo", [P, NG, D], F32)

        bank = [ctx.enter_context(nc.psum_tensor(f"bank{i}", [P, 512], F32)) for i in range(8)]
        TRANS, QB, KB, WOB, S0, S1, PTB, OTB = bank
        VB, PT1B, GATEB = S0, QB, KB

        names = ("x_in ln1_in consts_in tables wsplit scaled "
                 "st1_ready st2_ready mv_ready ve_ready "
                 "rstd_ready xn_ready xn2_ready xb_ready adj_cast adj_part adj_ready "
                 "xt_done xth_ready xtl_ready q_done k_done qh_ready ql_ready kh_ready kl_ready "
                 "kbd_in v_done va_ready vd_ready scores0 scores1 max0 max1 exp0 exp1 rs0 rs1 "
                 "norm0 norm1 pt0_done pt1_done pt0_ready pt1_ready av_done oth_ready otl_ready "
                 "wo_done x2_ready t2_done x2t_ready gate_done eg_ready eg1_ready sel_ready "
                 "top_ready topi_ready topf_ready oh_ready ch_ready rank_done rank_ready carry_ready "
                 "init_dve init_pool zero_out keys_in values_in "
                 "disp disp_pool row_out row_in xs_ready ln2_kept").split()
        s = {n: sem(n) for n in names}
        sc_out = [sem(f"sc_out{i}") for i in range(NSC)]
        s_e = {n: sem("e_" + n) for n in ("xgt_done xgt_ready hid_done hid_ready hidt_done hidt_ready "
                                           "y_done y_copied half_sum y_ready").split()}
        xg_in = [sem(f"xg_in{i}") for i in range(NX)]
        yb_out = [sem(f"yb_out{i}") for i in range(2)]
        ga_in = [sem(f"ga_in{i}") for i in range(NG)]
        yo_out = [sem(f"yo_out{i}") for i in range(NG)]
        CONSTS = 11
        DISP_END = []
        keys_flat = keys_sb[:].rearrange("p e c h -> p (e c h)")
        wqkv_stage = keys_flat[:, 0:FC * 3 * D].rearrange("p (c n) -> p c n", c=FC)
        wo_stage = keys_flat[:, FC * 3 * D:FC * 4 * D].rearrange("p (c n) -> p c n", c=FC)
        static_stage = keys_flat[:, 2048:2048 + 6 * SQ].rearrange("p (h t) -> p h t", h=6)
        before_stage = keys_flat[:, 3072:3072 + P]

        def wait(eng, name, count):
            if isinstance(count, int):
                if count > 0:
                    eng.wait_ge(s[name], count)
            else:
                eng.wait_ge(s[name], count)

        def wait_last(eng, name, count):
            wait(eng, name, min(count, UNITS) if isinstance(count, int) else count)

        def wait_apart(eng, *counts):
            counts = [(name, c if isinstance(c, int) else eng.snap(c)) for name, c in counts]
            eng.wait_ge(s["consts_in"], 16 * CONSTS)
            for name, c in counts:
                wait(eng, name, c)

        def live(u):
            return not isinstance(u, int) or 0 <= u < UNITS

        FIRST, LAST = 4, UNITS - 4

        def pipeline(eng, step):
            for n in range(-3, FIRST):
                step(n)
            with eng.Fori(FIRST, LAST + 1) as n:
                step(n)
            for n in range(LAST + 1, UNITS + 4):
                step(n)

        def experts(eng, step):
            for j in range(2):
                for k in range(NX):
                    step(j, k)
            with eng.Fori(2, BLOCKS // NX) as j:
                for k in range(NX):
                    step(j, k)
            for k in range(NX):
                step(BLOCKS // NX, k)
            step(BLOCKS // NX + 1, 0)

        x_tiles = x.rearrange("(t b) s d -> (b s) t d", b=2)
        adj_tiles = adj.rearrange("(t b) s k -> (b s) t k", b=2)
        out_tiles = out.rearrange("(t b) s d -> (b s) t d", b=2)

        def q_view(t, c):
            return t[:, c, :].rearrange("p (b y) -> p b y", y=P)[:, :, 0:SQ]

        def by_board(ap):
            return ap.rearrange("p (b y) -> p b y", y=SQ)

        block = ctx.enter_context(nc.Block())

        @block.sync
        def _(sp):
            def load_x(u):
                if live(u):
                    wait(sp, "x_in", 16 * u)
                    sp.dma_start(x_all[:, bass.ds(2 * u, 2), :],
                                 x_tiles[:, bass.ds(2 * u, 2), :]).then_inc(s["x_in"], 16)

            load_x(0)
            for dst, src in ((wqkv_stage, wqkv), (wo_stage, wo), (bias_sb[:], bqkv), (eye[:], c_eye),
                             (others[:], c_others), (static_stage, c_static),
                             (bo_sb[:], bo.rearrange("(a d) -> a d", a=1).broadcast_to([P, D])),
                             (adj_sb[:], adj_tiles), (sel_sb[:], sel), (before_stage, c_before),
                             (iota[:], c_iota)):
                sp.dma_start(dst, src).then_inc(s["consts_in"], 16)

            def step(n):
                u = n
                if live(u):
                    wait(sp, "init_pool", 1)
                    wait(sp, "kh_ready", u + 1)
                    wait(sp, "kl_ready", u + 1)
                    for dst, src in ((kbd_h, k_h), (kbd_l, k_l)):
                        for j in range(4):
                            r = slice(HD * j, HD * j + HD)
                            sp.dma_start(dst[r, :, j, :].bitcast(F32), src[r, :, :].bitcast(F32)).then_inc(s["kbd_in"], 16)
                load_x(n + 3)

            for n in range(-2, FIRST):
                step(n)
            with sp.Fori(FIRST, LAST + 1) as n:
                step(n)
            for n in range(LAST + 1, UNITS):
                step(n)

            wait(sp, "ch_ready", UNITS)
            wait(sp, "carry_ready", UNITS)
            sp.dma_start(values_sb[:], values).then_inc(s["values_in"], 16)

            for i in range(NSC):
                sp.wait_ge(sc_out[i], 32 * (TILES // NSC))
            sp.wait_ge(s["zero_out"], 160)

            def load_rows(b, k):
                sp.dma_start(xg[:, k, :], rows_in[bass.ds(b * P, P), :]).then_inc(xg_in[k], 16)

            for k in range(NX):
                load_rows(k, k)
            with sp.Fori(1, BLOCKS // NX) as j:
                for k in range(NX):
                    sp.wait_ge(s_e["xgt_done"], (j - 1) * NX + k + 1)
                    load_rows(j * NX + k, k)

            with sp.Fori(0, TILES // NG) as j:
                for k in range(NG):
                    sp.wait_ge(s_e["y_ready"], j * NG + k + 1)
                    sp.dma_start(out_tiles[:, bass.ds(j * NG + k, 1), :],
                                 yo[:, k:k + 1, :]).then_inc(yo_out[k], 16)
            for k in range(NG):
                sp.wait_ge(yo_out[k], 16 * (TILES // NG))

        @block.tensor
        def _(pe):
            def parts3(dst, lh, ll, rh, rl, start, stop, **kw):
                pe.matmul(dst, lh, rh, start=start, stop=False, **kw)
                pe.matmul(dst, ll, rh, start=False, stop=False, **kw)
                return pe.matmul(dst, lh, rl, start=False, stop=stop, **kw)

            def scores(u):
                if not live(u):
                    return
                wait(pe, "qh_ready", u + 1)
                wait(pe, "ql_ready", u + 1)
                wait(pe, "kbd_in", 128 * (u + 1))
                wait(pe, "adj_ready", u + 1)
                for i, S in enumerate((S0, S1)):
                    if i == 0:
                        wait(pe, "va_ready", u + 1)
                        wait(pe, "vd_ready", u + 1)
                    else:
                        wait(pe, "exp1", u)
                    adj2 = adj_bias[:, i, None, :].broadcast_to([P, 2, SQ])
                    pe.matmul(S[:, 0:384], eyeb[:], static_sb[:].rearrange("p h t -> p (h t)"),
                              start=True, stop=False, skip_group_check=True)
                    pe.matmul(S[:, 384:512], eyeb[:], adj2,
                              start=False, stop=False, skip_group_check=True)
                    for c in range(FC):
                        for b in range(2):
                            q0 = (2 * i + b) * P - b * SQ
                            k0 = i * P + b * SQ
                            mm = parts3(S[:, 256 * c:256 * c + 256],
                                        qz_h[:, c, q0:q0 + P], qz_l[:, c, q0:q0 + P],
                                        kbd_h[:, c, :, k0:k0 + SQ], kbd_l[:, c, :, k0:k0 + SQ],
                                        False, b == 1, skip_group_check=True)
                    mm.then_inc(s[f"scores{i}"], 1)

            def project_qk(u):
                if not live(u):
                    return
                wait(pe, "wsplit", 4)
                wait(pe, "xth_ready", u + 1)
                wait(pe, "xtl_ready", u + 1)
                for w, (B, done) in enumerate(((QB, "q_done"), (KB, "k_done"))):
                    if w == 0:
                        wait(pe, "pt1_ready", u - 1)
                    else:
                        wait(pe, "rank_ready", u - 3)
                        wait(pe, "carry_ready", u - 3)
                    for f in range(FC):
                        col = slice(w * D + f * P, w * D + f * P + P)
                        for c in range(FC):
                            mm = parts3(B[:, 256 * f:256 * f + 256],
                                        wqkv_h[:, c, col], wqkv_l[:, c, col],
                                        xt_h[:, c, :], xt_l[:, c, :], c == 0, c == FC - 1)
                    mm.then_inc(s[done], 1)

            def project_v(u):
                if not live(u):
                    return
                wait(pe, "exp0", u)
                for i in range(2):
                    tok = slice(i * P, i * P + P)
                    for c in range(FC):
                        mm = parts3(VB[:, D * i:D * i + D], xt_h[:, c, tok], xt_l[:, c, tok],
                                    wqkv_h[:, c, 2 * D:], wqkv_l[:, c, 2 * D:],
                                    c == 0, c == FC - 1)
                mm.then_inc(s["v_done"], 1)

            def transposed(src, done):
                for c in range(FC):
                    for i in range(2):
                        at = c * 2 * P + i * P
                        mm = pe.transpose(TRANS[:, at:at + P], src[:, i, c * P:c * P + P], eye[:])
                mm.then_inc(s[done], 1)

            def probs_turned(u, i):
                if not live(u):
                    return
                wait(pe, f"norm{i}", u + 1)
                if i == 0:
                    wait(pe, "pt0_ready", u)
                    B = PTB
                else:
                    wait_last(pe, "qh_ready", u + 2)
                    wait_last(pe, "ql_ready", u + 2)
                    B = PT1B
                for j in range(4):
                    mm = pe.transpose(B[:, j * P:j * P + P], probs[:, i, j * P:j * P + P], eye[:])
                mm.then_inc(s[f"pt{i}_done"], 1)

            def attend(u):
                if not live(u):
                    return
                wait(pe, "pt0_ready", u + 1)
                wait(pe, "pt1_ready", u + 1)
                wait(pe, "va_ready", u + 1)
                wait(pe, "vd_ready", u + 1)
                wait(pe, "oth_ready", u)
                wait(pe, "otl_ready", u)
                for i in range(2):
                    for j in range(4):
                        for b in range(2):
                            half_ = SQ * (j % 2)
                            col = (i * FC + j // 2) * P + b * SQ
                            mm = pe.matmul(OTB[half_:half_ + SQ, col:col + SQ],
                                           vbd[:, i, b, j, :, :].rearrange("p r c -> p (r c)"),
                                           probs_t[:, i, j * P + b * SQ:j * P + b * SQ + SQ],
                                           start=True, stop=True)
                mm.then_inc(s["av_done"], 1)

            def project_out(u):
                if not live(u):
                    return
                wait(pe, "oth_ready", u + 1)
                wait(pe, "otl_ready", u + 1)
                wait(pe, "x2_ready", u)
                for i in range(2):
                    for c in range(FC):
                        mm = parts3(WOB[:, D * i:D * i + D], ot_h[:, i, c, :], ot_l[:, i, c, :],
                                    wo_h[:, c, :], wo_l[:, c, :], c == 0, c == FC - 1)
                mm.then_inc(s["wo_done"], 1)

            def turn1(u):
                if live(u):
                    wait(pe, "consts_in", 16 * CONSTS)
                    wait(pe, "xn_ready", u + 1)
                    wait(pe, "x2t_ready", u - 2)
                    transposed(xn, "xt_done")

            def turn2(u):
                if live(u):
                    wait(pe, "xn2_ready", u + 1)
                    wait_last(pe, "xth_ready", u + 3)
                    wait_last(pe, "xtl_ready", u + 3)
                    transposed(xn2, "t2_done")

            def gates(u):
                if not live(u):
                    return
                wait(pe, "x2t_ready", u + 1)
                wait_last(pe, "kh_ready", u + 3)
                wait_last(pe, "kl_ready", u + 3)
                wait(pe, "rank_ready", u - 1)
                wait(pe, "carry_ready", u - 1)
                for i in range(2):
                    for b in range(2):
                        tok = i * P + b * SQ
                        for c in range(FC):
                            mm = pe.matmul(GATEB[b * SQ:b * SQ + SQ, i * EXPERTS:(i + 1) * EXPERTS],
                                           x2t[:, c, tok:tok + SQ], sel_sb[:, c, :],
                                           start=c == 0, stop=c == FC - 1)
                mm.then_inc(s["gate_done"], 1)

            def ranks(u):
                if not live(u):
                    return
                wait(pe, "ch_ready", u + 1)
                wait_last(pe, "eg_ready", u + 2)
                wait(pe, "carry_ready", u)
                a, b, c = (slice(64 + EXPERTS * k, 96 + EXPERTS * k) for k in range(3))
                pe.matmul(GATEB[:, a], before[:], chosen[:, 0, :], start=True, stop=True)
                pe.matmul(GATEB[:, b], onesb[:], chosen[:, 0, :], start=True, stop=False)
                pe.matmul(GATEB[:, b], before[:], chosen[:, 1, :], start=False, stop=True)
                pe.matmul(GATEB[:, c], onesb[:], chosen[:, 0, :], start=True, stop=False)
                pe.matmul(GATEB[:, c], onesb[:], chosen[:, 1, :], start=False, stop=True)\
                  .then_inc(s["rank_done"], 1)

            def step(n):
                scores(n - 1)
                project_qk(n)
                turn2(n - 2)
                probs_turned(n - 1, 0)
                gates(n - 2)
                probs_turned(n - 1, 1)
                attend(n - 1)
                project_v(n)
                turn1(n + 1)
                project_out(n - 1)
                ranks(n - 3)

            pe.wait_ge(s["tables"], 1)
            pe.wait_ge(s["init_dve"], 2)
            pe.wait_ge(s["init_pool"], 1)
            pipeline(pe, step)

            pe.wait_ge(s["values_in"], 16)
            pe.wait_ge(s["keys_in"], 16)
            pe.wait_ge(s["row_in"], 16)
            pe.wait_ge(s["carry_ready"], UNITS)

            def expert_step(j, k):
                n = j * NX + k

                def ok(b):
                    return not isinstance(b, int) or 0 <= b < BLOCKS

                def w(name, count):
                    if not (isinstance(count, int) and count <= 0):
                        pe.wait_ge(s_e[name], count)

                def owner_of(b):
                    return pe.value_load(owner_row[0:1, bass.ds(b, 1)], min_val=0, max_val=EXPERTS - 1)

                if ok(n):
                    q, B = k % 2, (bank[0], bank[1])[k % 2]
                    pe.wait_ge(xg_in[k], 16 * (j + 1))
                    w("xgt_ready", n - 1)
                    for c in range(FC):
                        mm = pe.transpose(B[:, c * P:c * P + P], xg[:, k % NX, c * P:c * P + P], eye[:])
                    mm.then_inc(s_e["xgt_done"], 1)
                if ok(n - 1):
                    q, B = (k - 1) % 2, (bank[2], bank[3])[(k - 1) % 2]
                    e = owner_of(n - 1)
                    w("xgt_ready", n)
                    w("hid_ready", n - 2)
                    for c in range(FC):
                        mm = pe.matmul(B[:, 0:HID], xgt[:, q, c, :], keys_sb[:, bass.ds(e, 1), c, :],
                                       start=c == 0, stop=c == FC - 1)
                    mm.then_inc(s_e["hid_done"], 1)
                if ok(n - 2):
                    q, B = k % 2, (bank[4], bank[5])[k % 2]
                    w("hid_ready", n - 1)
                    w("hidt_ready", n - 3)
                    pe.transpose(B[:, 0:P], hid[:, q, :], eye[:]).then_inc(s_e["hidt_done"], 1)
                if ok(n - 3):
                    q, B = (k - 1) % 2, (bank[6], bank[7])[(k - 1) % 2]
                    e = owner_of(n - 3)
                    w("hidt_ready", n - 2)
                    w("y_copied", n - 4)
                    pe.matmul(B[:, 0:D], hidt[:, q, :], values_sb[:, bass.ds(e, 1), :],
                              start=True, stop=True).then_inc(s_e["y_done"], 1)

            experts(pe, expert_step)

        @block.scalar
        def _(act):
            act.wait_ge(s["consts_in"], 16 * CONSTS)
            act.wait_ge(s["scaled"], 2)
            nc.scalar.activation(wqkv_h[:], wqkv_stage, ACT.Copy).then_inc(s["wsplit"], 1)
            nc.scalar.activation(wo_h[:], wo_stage, ACT.Copy).then_inc(s["wsplit"], 1)

            def softmax(u, i):
                if not live(u):
                    return
                wait(act, f"max{i}", u + 1)
                wait(act, f"pt{i}_done", u)
                S = (S0, S1)[i]
                for h in range(HEADS):
                    a = nc.scalar.activation(probs[:, i, h * SQ:h * SQ + SQ], S[:, h * SQ:h * SQ + SQ],
                                             ACT.Exp, bias=nmax[:, i, h:h + 1], scale=1.0,
                                             accum_out=psum_p[:, i, h:h + 1])
                a.then_inc(s[f"exp{i}"], 1)

            def step(n):
                softmax(n - 1, 0)
                softmax(n - 1, 1)
                if live(n):
                    wait(act, "q_done", n + 1)
                    wait(act, "init_pool", 1)
                    for f in range(FC):
                        a = nc.scalar.activation(q_view(qz_h, f), by_board(QB[:, 256 * f:256 * f + 256]),
                                                 ACT.Identity, bias=bq_s[:, f:f + 1], scale=1.0)
                    a.then_inc(s["qh_ready"], 1)
                    wait(act, "k_done", n + 1)
                    wait(act, "kbd_in", 128 * n)
                    for f in range(FC):
                        a = nc.scalar.activation(k_h[:, f, :], KB[:, 256 * f:256 * f + 256],
                                                 ACT.Identity, bias=bias_sb[:, 1, f:f + 1], scale=1.0)
                    a.then_inc(s["kh_ready"], 1)
                if live(n - 2):
                    wait(act, "t2_done", n - 1)
                    nc.scalar.activation(x2t[:].rearrange("p c t -> p (c t)"), TRANS[:], ACT.Copy)\
                        .then_inc(s["x2t_ready"], 1)
                if live(n - 1):
                    wait(act, "pt0_done", n)
                    nc.scalar.activation(probs_t[:, 0, :], PTB[:], ACT.Copy).then_inc(s["pt0_ready"], 1)
                if live(n - 2):
                    wait(act, "gate_done", n - 1)
                    wait(act, "eg1_ready", n - 2)
                    nc.scalar.activation(egate[:].rearrange("p i e -> p (i e)"), GATEB[:, 0:2 * EXPERTS],
                                         ACT.Exp, scale=-1.0).then_inc(s["eg_ready"], 1)
                if live(n - 1):
                    wait(act, "av_done", n)
                    for f in range(FC):
                        src = OTB[:].rearrange("p (i f t) -> p i f t", i=2, f=FC)[:, :, f, :]
                        a = nc.scalar.activation(ot_h[:, :, f, :], src, ACT.Identity,
                                                 bias=bias_sb[:, 2, f:f + 1], scale=1.0)
                    a.then_inc(s["oth_ready"], 1)
                if live(n):
                    wait(act, "v_done", n + 1)
                    src = VB[:].rearrange("p (i j r c) -> p i j r c", i=2, j=4, r=2)
                    for r in range(2):
                        a = nc.scalar.activation(vbd[SQ * r:SQ * r + SQ, :, 0, :, r, :], src[0:SQ, :, :, r, :],
                                                 ACT.Copy)
                    a.then_inc(s["va_ready"], 1)
                if live(n + 1):
                    wait(act, "xt_done", n + 2)
                    nc.scalar.activation(xt_h[:].rearrange("p c t -> p (c t)"), TRANS[:], ACT.Copy)\
                        .then_inc(s["xth_ready"], 1)

            act.wait_ge(s["init_pool"], 1)
            pipeline(act, step)

            act.wait_ge(s["values_in"], 16)

            def w(name, count):
                if not (isinstance(count, int) and count <= 0):
                    act.wait_ge(s_e[name], count)

            def expert_step(j, k):
                n = j * NX + k

                def ok(b):
                    return not isinstance(b, int) or 0 <= b < BLOCKS
                if ok(n):
                    w("xgt_done", n + 1)
                    w("hid_done", n - 1)
                    nc.scalar.activation(xgt[:, k % 2, :, :].rearrange("p c t -> p (c t)"),
                                         (bank[0], bank[1])[k % 2][:, 0:2 * P], ACT.Copy)\
                        .then_inc(s_e["xgt_ready"], 1)
                if ok(n - 2):
                    w("hidt_done", n - 1)
                    w("y_done", n - 3)
                    nc.scalar.activation(hidt[:, k % 2, :], (bank[4], bank[5])[k % 2][:, 0:P], ACT.Copy)\
                        .then_inc(s_e["hidt_ready"], 1)
                if ok(n - 4):
                    w("y_copied", n - 3)
                    act.dma_start(rows_out[bass.ds((n - 4) * P, P), :], yb[:, k % 2, :])\
                       .then_inc(yb_out[k % 2], 16)

            experts(act, expert_step)

        @block.vector
        def _(v):
            v.memset(onesb[:], 1.0).then_inc(s["init_dve"], 1)
            v.memset(minus_half[:], -0.5)
            v.memset(carry[:], 0.0).then_inc(s["init_dve"], 1)
            v.wait_ge(s["consts_in"], 16 * CONSTS)
            v.tensor_scalar(wqkv_stage[:, :, 0:D], wqkv_stage[:, :, 0:D], SCALE, None, ALU.mult)\
             .then_inc(s["scaled"], 1)
            v.tensor_copy(static_sb[:], static_stage)
            v.tensor_copy(before[:], before_stage)
            v.tensor_copy(eyeb[:], eye[:]).then_inc(s["tables"], 1)
            v.tensor_scalar(bq_s[:], bias_sb[:, 0, :], SCALE, None, ALU.mult).then_inc(s["scaled"], 1)
            v.wait_ge(s["scaled"], 2)
            v.wait_ge(s["wsplit"], 2)
            v.tensor_tensor(wqkv_l[:], wqkv_stage, wqkv_h[:].bitcast(F32), ALU.subtract)\
             .then_inc(s["wsplit"], 1)
            v.tensor_tensor(wo_l[:], wo_stage, wo_h[:].bitcast(F32), ALU.subtract)\
             .then_inc(s["wsplit"], 1)

            def stats(n):
                a, b = (live(n + 2), live(n - 1))
                if not (a or b):
                    return
                if b:
                    wait_apart(v, ("x2_ready", n))
                    for i in range(2):
                        ins = v.bn_stats(st2[:, i, :], x_all[:, bass.ds(2 * (n - 1) + i, 1), :]
                                         .rearrange("p a d -> p (a d)"))
                    ins.then_inc(s["st2_ready"], 1)
                if a:
                    wait_apart(v, ("x_in", 16 * (n + 3)))
                    for i in range(2):
                        ins = v.bn_stats(st1[:, i, :], x_all[:, bass.ds(2 * (n + 2) + i, 1), :]
                                         .rearrange("p a d -> p (a d)"))
                    ins.then_inc(s["st1_ready"], 1)
                counts = [("ln2_kept", n - 1)]
                if a:
                    counts.append(("st1_ready", n + 3))
                if b:
                    counts.append(("st2_ready", n))
                if live(n + 1) or live(n - 2):
                    counts.append(("rstd_ready", n + 2))
                wait_apart(v, *counts)
                if a:
                    for i in range(2):
                        ins = v.bn_aggr(mv[:, i, :], st1[:, i, :])
                if b:
                    for i in range(2):
                        ins = v.bn_aggr(mv[:, 2 + i, :], st2[:, i, :])
                ins.then_inc(s["mv_ready"], 1)
                wait(v, "mv_ready", n + 3)
                lo, hi = (0 if a else 2), (4 if b else 2)
                v.tensor_scalar(ve[:, lo:hi], mv[:, lo:hi, 1], EPS, None, ALU.add)\
                 .then_inc(s["ve_ready"], 1)

            def split_low(done, waits, items):
                for name, count in waits:
                    wait(v, name, count)
                for dst, src, bias, high in items:
                    ins = v.scalar_tensor_tensor(dst, src, bias, high, ALU.add, ALU.subtract)
                ins.then_inc(s[done], 1)

            def normalise(dst, u, at, done):
                for i in range(2):
                    ins = v.tensor_scalar(dst[:, i, :], x_all[:, bass.ds(2 * u + i, 1), :]
                                          .rearrange("p a d -> p (a d)"),
                                          mv[:, at + i, 0:1], rstd[:, at + i:at + i + 1],
                                          ALU.subtract, ALU.mult)
                ins.then_inc(s[done], 1)

            def step(n):
                if live(n - 2):
                    wait(v, "rstd_ready", n + 2)
                    wait(v, "t2_done", n - 2)
                    normalise(xn2, n - 2, 2, "xn2_ready")
                if live(n - 1):
                    for i, S in enumerate((S0, S1)):
                        wait(v, f"scores{i}", n)
                        v.tensor_reduce(nmax[:, i, :], S[:].rearrange("p (h t) -> p h t", h=HEADS),
                                        AX.X, ALU.max, negate=True).then_inc(s[f"max{i}"], 1)
                    for i in range(2):
                        wait(v, f"exp{i}", n)
                        wait(v, f"norm{i}", n - 1)
                        v.reciprocal(rsum[:, i, :], psum_p[:, i, :]).then_inc(s[f"rs{i}"], 1)
                if live(n + 1):
                    wait(v, "rstd_ready", n + 2)
                    wait(v, "xt_done", n + 1)
                    normalise(xn, n + 1, 0, "xn_ready")
                if live(n):
                    split_low("ql_ready", [("qh_ready", n + 1)],
                              [(q_view(qz_l, f), by_board(QB[:, 256 * f:256 * f + 256]),
                                bq_s[:, f:f + 1], q_view(qz_h, f).bitcast(F32)) for f in range(FC)])
                    split_low("kl_ready", [("kh_ready", n + 1)],
                              [(k_l[:, f, :], KB[:, 256 * f:256 * f + 256], bias_sb[:, 1, f:f + 1],
                                k_h[:, f, :].bitcast(F32)) for f in range(FC)])
                if live(n - 1):
                    wait(v, "pt1_done", n)
                    v.tensor_copy(probs_t[:, 1, :], PT1B[:]).then_inc(s["pt1_ready"], 1)
                if live(n - 2):
                    route(n - 2)
                if live(n - 1):
                    src = OTB[:].rearrange("p (i f t) -> p i f t", i=2, f=FC)
                    split_low("otl_ready", [("oth_ready", n)],
                              [(ot_l[:, :, f, :], src[:, :, f, :], bias_sb[:, 2, f:f + 1],
                                ot_h[:, :, f, :].bitcast(F32)) for f in range(FC)])
                if live(n):
                    wait(v, "v_done", n + 1)
                    src = VB[:].rearrange("p (i j r c) -> p i j r c", i=2, j=4, r=2)
                    for r in range(2):
                        ins = v.tensor_copy(vbd[SQ * r:SQ * r + SQ, :, 1, :, r, :], src[SQ:P, :, :, r, :])
                    ins.then_inc(s["vd_ready"], 1)
                if live(n + 1):
                    wait(v, "xth_ready", n + 2)
                    v.tensor_tensor(xt_l[:].rearrange("p c t -> p (c t)"), TRANS[:],
                                    xt_h[:].bitcast(F32).rearrange("p c t -> p (c t)"), ALU.subtract)\
                     .then_inc(s["xtl_ready"], 1)
                if live(n - 1):
                    wait(v, "wo_done", n)
                    wait(v, "xb_ready", n)
                    tiles = x_all[:, bass.ds(2 * (n - 1), 2), :]
                    v.tensor_tensor(tiles, WOB[:].rearrange("p (i d) -> p i d", i=2), tiles, ALU.add)\
                     .then_inc(s["x2_ready"], 1)
                stats(n)
                if live(n - 3):
                    wait(v, "rank_done", n - 2)
                    wait(v, "carry_ready", n - 3)
                    v.tensor_tensor(rank_all[:, bass.ds(2 * (n - 3), 2), :],
                                    GATEB[:, 64:64 + 2 * EXPERTS].rearrange("p (i e) -> p i e", i=2),
                                    carry[:, None, :].broadcast_to([P, 2, EXPERTS]), ALU.add)\
                     .then_inc(s["rank_ready"], 1)
                    wait(v, "rank_ready", n - 2)
                    v.tensor_tensor(carry[:], GATEB[:, 128:128 + EXPERTS], carry[:], ALU.add)\
                     .then_inc(s["carry_ready"], 1)

            def route(u):
                wait(v, "eg_ready", u + 1)
                wait(v, "sel_ready", u)
                v.tensor_scalar(egate1[:], egate[:], 1.0, None, ALU.add).then_inc(s["eg1_ready"], 1)
                wait(v, "eg1_ready", u + 1)
                wait(v, "topi_ready", u)
                v.reciprocal(gate[:], egate1[:]).then_inc(s["sel_ready"], 1)
                wait_apart(v, ("sel_ready", u + 1))
                for i in range(2):
                    ins = v.max(top[:, i, :], gate[:, i, :])
                ins.then_inc(s["top_ready"], 1)
                wait(v, "top_ready", u + 1)
                v.tensor_copy(top_all[:, bass.ds(2 * u, 2), :], top[:, :, 0:2])
                wait_apart(v, ("topf_ready", u))
                for i in range(2):
                    ins = v.max_index(topi[:, i, :], top[:, i, :], gate[:, i, :])
                ins.then_inc(s["topi_ready"], 1)

            v.wait_ge(s["wsplit"], 4)
            pipeline(v, step)

            count = [0]

            def link(ins):
                count[0] += 1
                ins.then_inc(s["disp"], 1)
                v.wait_ge(s["disp"], count[0])

            v.wait_ge(s["carry_ready"], UNITS)
            v.wait_ge(s["ch_ready"], UNITS)
            link(v.tensor_scalar(blocksi[:, 0, :], carry[:], float(P - 1), None, ALU.add))
            link(v.tensor_scalar(blocksi[:, 1, :], blocksi[:, 0, :], 7, None, ALU.logical_shift_right))
            link(v.tensor_copy(blocksf[:], blocksi[:, 1, :]))
            link(v.tensor_copy(cum[:, 0, :], blocksf[:]))
            at, k = 0, 1
            while k < EXPERTS:
                link(v.tensor_copy(cum[:, 1 - at, 0:k], cum[:, at, 0:k]))
                link(v.tensor_tensor(cum[:, 1 - at, k:], cum[:, at, k:], cum[:, at, 0:EXPERTS - k],
                                     ALU.add))
                at, k = 1 - at, 2 * k
            link(v.tensor_tensor(base[:], cum[:, at, :], blocksf[:], ALU.subtract))
            link(v.tensor_scalar(base[:], base[:], float(P), None, ALU.mult))
            for r in range(2):
                link(v.tensor_scalar(below[:, r, :], cum[:, at, :], pidxf[:, r:r + 1], None, ALU.is_le))
            link(v.tensor_reduce(owner[:], below[:], AX.X, ALU.add))
            link(v.tensor_scalar(owneri[:], owner[:], float(EXPERTS - 1), None, ALU.min))
            link(v.tensor_tensor(rank_all[:], rank_all[:],
                                 base[:, None, :].broadcast_to([P, TILES, EXPERTS]), ALU.add))
            for half_ in range(4):
                ts = slice(half_ * TILES // 4, (half_ + 1) * TILES // 4)
                n4 = TILES // 4
                sp4 = spread[:].rearrange("p t k e -> p (t k e)")[:, 0:n4 * 2 * EXPERTS]\
                    .rearrange("p (t k e) -> p t k e", t=n4, k=2)
                link(v.tensor_tensor(sp4, onehot[:, ts, :, :],
                                     rank_all[:, ts, None, :].broadcast_to([P, n4, 2, EXPERTS]),
                                     ALU.mult))
                link(v.tensor_reduce(slotf[:, half_ * 2 * n4:(half_ + 1) * 2 * n4],
                                     sp4.rearrange("p t k e -> p (t k) e"), AX.X, ALU.add))
            link(v.tensor_copy(slot[:], slotf[:]))
            DISP_END.append(count[0])

            def row_to_scatter(j, k):
                t = j * NSC + k
                if not (isinstance(j, int) and j == 0):
                    v.wait_ge(sc_out[k], 32 * j)
                v.tensor_scalar(xs[:, k, :], x_all[:, bass.ds(t, 1), :].rearrange("p a d -> p (a d)"),
                                ln2_all[:, bass.ds(t, 1), 0], ln2_all[:, bass.ds(t, 1), 1],
                                ALU.subtract, ALU.mult).then_inc(s["xs_ready"], 1)

            for k in range(NSC):
                row_to_scatter(0, k)
            with v.Fori(1, TILES // NSC) as j:
                for k in range(NSC):
                    row_to_scatter(j, k)

            v.wait_ge(s["values_in"], 16)

            def w(name, count):
                if not (isinstance(count, int) and count <= 0):
                    v.wait_ge(s_e[name], count)

            def expert_step(j, k):
                n = j * NX + k

                def ok(b):
                    return not isinstance(b, int) or 0 <= b < BLOCKS
                if ok(n - 1):
                    q = (k - 1) % 2
                    w("hid_done", n)
                    w("hidt_done", n - 2)
                    v.tensor_scalar(hid[:, q, :], (bank[2], bank[3])[q][:, 0:HID], 0.0, None, ALU.max)\
                     .then_inc(s_e["hid_ready"], 1)
                if ok(n - 3):
                    q = (k - 1) % 2
                    w("y_done", n - 2)
                    stored = j * (NX // 2) + (k - 3 - q) // 2
                    if not (isinstance(stored, int) and stored <= 0):
                        v.wait_ge(yb_out[q], 16 * stored)
                    v.tensor_copy(yb[:, q, :], (bank[6], bank[7])[q][:, 0:D]).then_inc(s_e["y_copied"], 1)

            experts(v, expert_step)

            def combine(j, k):
                t = j * NG + k
                v.wait_ge(ga_in[k], 32 * (j + 1))
                if not (isinstance(j, int) and j == 0):
                    v.wait_ge(yo_out[k], 16 * j)
                v.scalar_tensor_tensor(ga[:, k, 0, :], ga[:, k, 0, :], top_all[:, bass.ds(t, 1), 0],
                                       x_all[:, bass.ds(t, 1), :].rearrange("p a d -> p (a d)"),
                                       ALU.mult, ALU.add).then_inc(s_e["half_sum"], 1)
                v.wait_ge(s_e["half_sum"], t + 1)
                v.scalar_tensor_tensor(yo[:, k, :], ga[:, k, 1, :], top_all[:, bass.ds(t, 1), 1],
                                       ga[:, k, 0, :], ALU.mult, ALU.add).then_inc(s_e["y_ready"], 1)

            for k in range(NG):
                combine(0, k)
            with v.Fori(1, TILES // NG) as j:
                for k in range(NG):
                    combine(j, k)

        @block.gpsimd
        def _(pool):
            g = nc.gpsimd
            g.memset(zeros[:], 0.0)
            for t in (kbd_h, kbd_l, qz_h, qz_l):
                g.memset(t[:].bitcast(F32), 0.0)
            g.memset(vbd[:], 0.0)
            g.iota(pidx[:], pattern=[[1, 2]], base=0, channel_multiplier=2).then_inc(s["init_pool"], 1)
            pool.wait_ge(s["init_pool"], 1)
            g.tensor_copy(pidxf[:], pidx[:]).then_inc(s["disp_pool"], 1)
            pool.wait_ge(s["init_dve"], 2)
            per = ROWS // P // 10
            padded = rows_in.rearrange("(p r) d -> p r d", p=P)
            for r in range(10):
                pool.dma_start(padded[:, r * per:(r + 1) * per, :],
                               zeros[:, None, :].broadcast_to([P, per, D])).then_inc(s["zero_out"], 16)
            pool.wait_ge(s["wsplit"], 4)
            pool.dma_start(keys_sb[:], keys).then_inc(s["keys_in"], 16)
            pool.wait_ge(s["consts_in"], 16 * CONSTS)

            def deviations(n):
                a, b = live(n + 1), live(n - 2)
                if not (a or b):
                    return
                lo, hi = (0 if a else 2), (4 if b else 2)
                wait(pool, "ve_ready", n + 2)
                wait_last(pool, "xn_ready", n + 1)
                wait(pool, "xn2_ready", n - 2)
                wait_last(pool, "x2_ready", n - 1)
                g.tensor_tensor(rstd[:, lo:hi], ve[:, lo:hi], minus_half[:, lo:hi], ALU.pow)\
                 .then_inc(s["rstd_ready"], 1)

            def step(n):
                deviations(n)
                if live(n - 2):
                    u = n - 2
                    g.tensor_copy(ln2_all[:, bass.ds(2 * u, 2), 0], mv[:, 2:4, 0])
                    wait_apart(pool, ("rstd_ready", n + 2))
                    g.tensor_copy(ln2_all[:, bass.ds(2 * u, 2), 1], rstd[:, 2:4]).then_inc(s["ln2_kept"], 1)
                if live(n - 1):
                    for i in range(2):
                        wait(pool, f"rs{i}", n)
                        pr = probs[:, i, :].rearrange("p (h t) -> p h t", h=HEADS)
                        g.tensor_tensor(pr, pr, rsum[:, i, :, None].broadcast_to([P, HEADS, SQ]), ALU.mult)\
                         .then_inc(s[f"norm{i}"], 1)
                if live(n + 1):
                    u = n + 1
                    wait(pool, "xn_ready", u + 1)
                    tiles = x_all[:, bass.ds(2 * u, 2), :]
                    g.tensor_tensor(tiles, tiles, bo_sb[:, None, :].broadcast_to([P, 2, D]), ALU.add)\
                     .then_inc(s["xb_ready"], 1)
                if live(n):
                    u = n
                    others2 = others[:, None, :].broadcast_to([P, 2, SQ])
                    g.tensor_copy(adj_f[:], adj_sb[:, bass.ds(2 * u, 2), :]).then_inc(s["adj_cast"], 1)
                    wait(pool, "adj_cast", u + 1)
                    g.tensor_tensor(adj_f[:], adj_f[:], others2, ALU.mult).then_inc(s["adj_part"], 1)
                    wait(pool, "adj_part", u + 1)
                    wait(pool, "scores1", u)
                    g.tensor_tensor(adj_bias[:], others2, adj_f[:], ALU.subtract)\
                     .then_inc(s["adj_ready"], 1)
                if live(n - 2):
                    u = n - 2
                    wait_apart(pool, ("topi_ready", u + 1))
                    g.tensor_copy(topf[:], topi[:, :, 0:2]).then_inc(s["topf_ready"], 1)
                    wait_apart(pool, ("topf_ready", u + 1), ("ch_ready", u))
                    for i in range(2):
                        for c in range(2):
                            ins = g.tensor_scalar(picks[:, i, c, :], iota[:], topf[:, i, c:c + 1], None,
                                                  ALU.is_equal)
                    ins.then_inc(s["oh_ready"], 1)
                    wait_apart(pool, ("oh_ready", u + 1))
                    g.tensor_copy(onehot[:, bass.ds(2 * u, 2), :, :], picks[:])
                    wait(pool, "rank_done", u)
                    g.tensor_tensor(chosen[:], picks[:, :, 0, :], picks[:, :, 1, :], ALU.add)\
                     .then_inc(s["ch_ready"], 1)

            pipeline(pool, step)

            pool.wait_ge(s["disp"], DISP_END[0])
            pool.dma_start(block_row.rearrange("(p r) -> p r", p=P), owneri[:]).then_inc(s["row_out"], 16)
            pool.wait_ge(s["row_out"], 16)
            pool.dma_start(owner_row[:], block_row.rearrange("(a r) -> a r", a=1)).then_inc(s["row_in"], 16)
            pool.wait_ge(s["zero_out"], 160)
            for t in range(TILES):
                pool.wait_ge(s["xs_ready"], t + 1)
                for c in range(2):
                    pool.indirect_dma_start(
                        rows_in, bass.IndirectOffsetOnAxis(ap=slot[:, 2 * t + c:2 * t + c + 1], axis=0),
                        xs[:, t % NSC, :], None).then_inc(sc_out[t % NSC], 16)

            for q in range(2):
                pool.wait_ge(yb_out[q], 16 * (BLOCKS // 2))
            for t in range(TILES):
                if t >= NG:
                    pool.wait_ge(s_e["y_ready"], t - NG + 1)
                for c in range(2):
                    pool.indirect_dma_start(
                        ga[:, t % NG, c, :], None, rows_out,
                        bass.IndirectOffsetOnAxis(ap=slot[:, 2 * t + c:2 * t + c + 1], axis=0))\
                        .then_inc(ga_in[t % NG], 16)


def kernel(**inputs):
    import numpy as np
    import concourse.bacc as bacc
    from concourse.bass_utils import run_bass_kernel_spmd

    def chunks(a):
        return np.ascontiguousarray(a.reshape(FC, P, -1).transpose(1, 0, 2))

    a = {k: np.asarray(v) for k, v in inputs.items()}
    arrays = {
        "x": a["x"],
        "adj": a["adj"],
        "wqkv": chunks(np.concatenate([a["L0_gnn_Wq"].T, a["L0_gnn_Wk"].T, a["L0_gnn_Wv"].T], axis=1)),
        "wo": chunks(a["L0_gnn_Wo"].T),
        "bqkv": np.ascontiguousarray(np.stack([a["L0_gnn_bq"], a["L0_gnn_bk"], a["L0_gnn_bv"]])
                                     .reshape(3, FC, P).transpose(2, 0, 1)),
        "bo": a["L0_gnn_bo"],
        "sel": chunks(a["L0_ffn_expert_sel"].T),
        "keys": np.ascontiguousarray(a["L0_ffn_keys"].reshape(EXPERTS, FC, P, HID).transpose(2, 0, 1, 3)),
        "values": np.ascontiguousarray(a["L0_ffn_values"].transpose(1, 0, 2)),
        **constants(),
    }
    nc = bacc.Bacc("TRN2", target_bir_lowering=False, num_devices=1)
    args = {k: nc.dram_tensor(f"in_{k}", v.shape, mybir.dt.from_np(v.dtype), kind="ExternalInput").ap()
            for k, v in arrays.items()}
    out = nc.dram_tensor("out_y", (BOARDS, SQ, D), F32, kind="ExternalOutput").ap()
    build(nc, out=out, **args)
    r = run_bass_kernel_spmd(nc, [{f"in_{k}": v for k, v in arrays.items()}], core_ids=[0])
    return r.results[0]["out_y"]
```

```python
from contextlib import ExitStack

import concourse.bass as bass
from concourse import mybir

F32 = mybir.dt.float32
F32R = mybir.dt.float32r
BF16 = mybir.dt.bfloat16
I32 = mybir.dt.int32
U32 = mybir.dt.uint32
U8 = mybir.dt.uint8
ALU = mybir.AluOpType
ACT = mybir.ActivationFunctionType
AX = mybir.AxisListType

P = 128
BOARDS, SQ, D = 128, 64, 256
HEADS = 8
HD = D // HEADS
EXPERTS, HID = 32, 128
TOKENS = BOARDS * SQ
TILES = TOKENS // P
UNITS = TILES // 2
FC = D // P
SCALE = HD ** -0.5
EPS = 1e-5
MASKED = -1e9
HALVES = 2
HALF_BLOCKS = 2 * TOKENS // HALVES // P + EXPERTS
BLOCKS = HALVES * HALF_BLOCKS
CAP = TOKENS // HALVES + P
SPARES = 4
ROWS = EXPERTS * CAP + SPARES * P
ROW = D + 2
DEST, GATE = D, D + 1
TAILS = 8
RESULTS = 2 * TOKENS + (SPARES + TAILS) * P
QPAD = 4 * P


def static_masks():
    import numpy as np
    sq = np.arange(SQ)
    r, f = sq // 8, sq % 8
    ri, rj, fi, fj = r[:, None], r[None, :], f[:, None], f[None, :]
    dr, df = np.abs(ri - rj), np.abs(fi - fj)
    eye = np.eye(SQ, dtype=bool)
    masks = [fi == fj, ri == rj, ri - fi == rj - fj, ri + fi == rj + fj,
             ((dr == 2) & (df == 1)) | ((dr == 1) & (df == 2)) | eye, (dr <= 1) & (df <= 1)]
    bias = np.where(np.stack(masks, 1), 0.0, MASKED)
    return np.concatenate([bias, bias]).astype(np.float32)


def constants():
    import numpy as np
    eye = np.eye(P, dtype=np.float32)
    return {
        "c_static": static_masks(),
        "c_eye": eye,
        "c_others": np.concatenate([np.where(np.eye(SQ), 0, MASKED).astype(np.float32)] * 2),
        "c_before": np.triu(np.ones((P, P), np.float32), 1),
        "c_iota": np.tile(np.arange(EXPERTS, dtype=np.float32), (P, 1)),
    }


def build(nc, x, adj, wqkv, wo, bqkv, bo, sel, keys, values, c_static, c_eye, c_others,
          c_before, c_iota, out):
    ctx = ExitStack()
    with ctx:
        def sb(name, shape, dt, where=ctx):
            return where.enter_context(nc.sbuf_tensor(name, shape, dt))

        def sem(name):
            return ctx.enter_context(nc.semaphore(name))

        rows_in = [nc.dram_tensor(f"rows_in{h}", (ROWS, ROW), F32).ap() for h in range(HALVES)]
        results = nc.dram_tensor("results", (RESULTS, D), F32).ap()
        block_tab = nc.dram_tensor("block_tab", (2, BLOCKS), I32).ap()

        x_all = sb("x_all", [P, TILES, D], F32)
        keys_sb = sb("keys_sb", [P, EXPERTS, FC, HID], F32)
        adj_sb = sb("adj_sb", [P, TILES, SQ], U8)
        static_sb = sb("static_sb", [P, 6, SQ], BF16)
        eye = sb("eye", [P, P], F32)
        eyeb = sb("eyeb", [P, P], BF16)
        before = sb("before", [P, P], BF16)
        onesb = sb("onesb", [P, P], BF16)
        iota = sb("iota", [P, EXPERTS], F32)
        round_up = sb("round_up", [P, EXPERTS], F32)
        ones_f = sb("ones_f", [P, EXPERTS], F32)
        sparei = sb("sparei", [P, 1], I32)
        spare = sb("spare", [P, 1], F32)
        pidx = sb("pidx", [P, 1], I32)
        pidxf = sb("pidxf", [P, 1], F32)
        zrow = sb("zrow", [P, TAILS, ROW], F32)
        xrow = sb("xrow", [P, 4, 2, 2, ROW], F32)
        slot = sb("slot", [P, 2, 4], I32)
        carry = sb("carry", [P, HALVES, EXPERTS], F32)
        place = sb("place", [P, 16 + SPARES + TAILS], I32)
        ends = sb("ends", [P, HALVES, EXPERTS], I32)
        AHEAD = 4
        expert_of = sb("expert_of", [1, AHEAD + BLOCKS + 8], I32)

        early = ExitStack()
        wqkv_h = sb("wqkv_h", [P, FC, 3 * D], F32R, early)
        wqkv_l = sb("wqkv_l", [P, FC, 3 * D], F32R, early)
        kbd = sb("kbd", [P, 2, FC, 4, 2 * P], F32R, early)
        qz_h = sb("qz_h", [P, FC, QPAD], F32R, early)
        qz_l = sb("qz_l", [P, FC, QPAD], F32R, early)
        k_hl = sb("k_hl", [P, 2, FC, 2 * P], F32R, early)
        xt_h = sb("xt_h", [P, FC, 2 * P], F32R, early)
        xt_l = sb("xt_l", [P, FC, 2 * P], F32R, early)
        wo_h = sb("wo_h", [P, FC, D], F32R, early)
        wo_l = sb("wo_l", [P, FC, D], F32R, early)
        vbd = sb("vbd", [P, 2, 2, 2, 4, 2, HD], F32, early)
        probs = sb("probs", [P, 2, 512], F32, early)
        probs_t = sb("probs_t", [P, 2, 512], F32, early)
        ot_h = sb("ot_h", [P, 2, FC, P], F32R, early)
        ot_l = sb("ot_l", [P, 2, FC, P], F32R, early)
        xn = sb("xn", [P, 2, D], F32, early)
        ones_r = sb("ones_r", [P, P], F32R, early)
        bo_rows = sb("bo_rows", [P, D], F32R, early)
        rank_row = sb("rank_row", [P, 2, EXPERTS], F32, early)
        slots_by = sb("slots_by", [P, 2, 2, EXPERTS], F32, early)
        x2t = sb("x2t", [P, FC, 2 * P], F32, early)
        sel_sb = sb("sel_sb", [P, FC, EXPERTS], F32, early)
        bias_sb = sb("bias_sb", [P, 3, FC], F32, early)
        bq_s = sb("bq_s", [P, FC], F32, early)
        others = sb("others", [P, SQ], F32, early)
        adj_f = sb("adj_f", [P, 2, SQ], F32, early)
        adj_bias = sb("adj_bias", [P, 2, SQ], BF16, early)
        st1 = sb("st1", [P, 2, 6], F32, early)
        st2 = sb("st2", [P, 2, 6], F32, early)
        mv = sb("mv", [P, 4, 2], F32, early)
        ve = sb("ve", [P, 4], F32, early)
        minus_half = sb("minus_half", [P, 4], F32, early)
        rstd = sb("rstd", [P, 4], F32, early)
        nmax = sb("nmax", [P, 2, HEADS], F32, early)
        psum_p = sb("psum_p", [P, 2, HEADS], F32, early)
        rsum = sb("rsum", [P, 2, HEADS], F32, early)
        egate = sb("egate", [P, 2, EXPERTS], F32, early)
        egate1 = sb("egate1", [P, 2, EXPERTS], F32, early)
        gate = sb("gate", [P, 2, EXPERTS], F32, early)
        top = sb("top", [P, 2, 8], F32, early)
        topi = sb("topi", [P, 2, 8], U32, early)
        topf = sb("topf", [P, 2, 2], F32, early)
        picks = sb("picks", [P, 2, 2, EXPERTS], BF16, early)
        chosen = sb("chosen", [P, 2, EXPERTS], BF16, early)
        early.close()
        values_sb = sb("values_sb", [P, EXPERTS, D], F32)
        blocksi = sb("blocksi", [P, 2, EXPERTS], I32)
        blocksf = sb("blocksf", [P, EXPERTS], F32)
        cum = sb("cum", [P, EXPERTS], F32)
        below = sb("below", [P, EXPERTS], F32)
        owned = sb("owned", [P, EXPERTS], F32)
        owner = sb("owner", [P, 1], F32)
        first = sb("first", [P, 1], F32)
        start = sb("start", [P, 1], F32)
        in_spares = sb("in_spares", [P, 1], F32)
        tab = sb("tab", [P, 2, HALVES], I32)
        start_of = sb("start_of", [1, BLOCKS], I32)
        NX = 8
        NY = 4
        xg = sb("xg", [P, NX, ROW], F32)
        meta = sb("meta", [P, NX, 2], F32)
        dest = sb("dest", [P, NX], I32)
        xgt = sb("xgt", [P, 2, FC, P], F32)
        hid = sb("hid", [P, 2, HID], F32)
        hidt = sb("hidt", [P, 2, P], F32)
        yb = sb("yb", [P, NY, D], F32)
        NG = 4
        ga = sb("ga", [P, NG, 2, 2, D], F32)
        yo = sb("yo", [P, NG, 2, D], F32)

        bank = [ctx.enter_context(nc.psum_tensor(f"bank{i}", [P, 512], F32)) for i in range(8)]
        TRANS, QB, KB, WOB, S0, S1, PTB, OTB = bank
        VB, PT1B, GATEB = S0, QB, KB

        names = ("x_in ln1_in consts_in tables wsplit scaled "
                 "st1_ready st2_ready mv_ready ve_ready "
                 "rstd_ready xn_ready xn2_ready adj_cast adj_part adj_ready "
                 "xt_done xth_ready xtl_ready q_done k_done qh_ready ql_ready kh_ready kl_ready "
                 "kbd_in v_done va_ready vd_ready scores0 scores1 max0 max1 exp0 exp1 rs0 rs1 "
                 "norm0 norm1 pt0_done pt1_done pt0_ready pt1_ready av_done oth_ready otl_ready "
                 "wo_done x2_ready t2_done x2t_ready gate_done eg_ready eg1_ready sel_ready "
                 "top_ready topi_ready topf_ready oh_ready ch_ready rank_done rank_ready carry_ready "
                 "init_dve init_pool spare_made bo_made zrow_ready spares_out keys_in values_in "
                 "disp disp_pool owned_ready ends_ready tab_ready tab_out tab_in slots_by_ready slot_ready dest_ready gate_kept").split()
        s = {n: sem(n) for n in names}
        sc_out = [sem(f"sc_out{i}") for i in range(4)]
        s_e = {n: sem("e_" + n) for n in ("xgt_done xgt_ready hid_done hid_ready hidt_done hidt_ready "
                                           "y_done y_copied meta_ready scattered both_sum y_ready").split()}
        row_copy = [sem(f"row_copy{i}") for i in range(4)]
        tails_out = [sem(f"tails_out{h}") for h in range(HALVES)]
        xg_in = [sem(f"xg_in{i}") for i in range(NX)]
        yb_out = [sem(f"yb_out{i}") for i in range(NY)]
        ga_in = [sem(f"ga_in{i}") for i in range(NG)]
        yo_out = [sem(f"yo_out{i}") for i in range(NG)]
        CONSTS = 11
        keys_flat = keys_sb[:].rearrange("p e c h -> p (e c h)")
        wqkv_stage = keys_flat[:, 0:FC * 3 * D].rearrange("p (c n) -> p c n", c=FC)
        wo_stage = keys_flat[:, FC * 3 * D:FC * 4 * D].rearrange("p (c n) -> p c n", c=FC)
        static_stage = keys_flat[:, 2048:2048 + 6 * SQ].rearrange("p (h t) -> p h t", h=6)
        before_stage = keys_flat[:, 3072:3072 + P]
        bo_sb, bo_h, bo_part = (keys_flat[:, 4096 + i * D:4096 + (i + 1) * D] for i in range(3))

        def wait(eng, name, count):
            if isinstance(count, int):
                if count > 0:
                    eng.wait_ge(s[name], count)
            else:
                eng.wait_ge(s[name], count)

        def wait_last(eng, name, count):
            wait(eng, name, min(count, UNITS) if isinstance(count, int) else count)

        def wait_apart(eng, *counts):
            counts = [(name, c if isinstance(c, int) else eng.snap(c)) for name, c in counts]
            eng.wait_ge(s["consts_in"], 16 * CONSTS)
            for name, c in counts:
                wait(eng, name, c)

        def live(u):
            return not isinstance(u, int) or 0 <= u < UNITS

        FIRST, LAST = 8, UNITS - 5

        def pipeline(eng, step, rounds=range(-3, UNITS + 5), after=None):
            for n in range(rounds[0], FIRST):
                step(n, n % 4, n // 4)
            with eng.Fori(FIRST // 4, (LAST + 1) // 4) as j:
                for k in range(4):
                    step(j * 4 + k, k, j)
            for n in range(LAST + 1, rounds[-1] + 1):
                step(n, n % 4, n // 4)
                if after and n in after:
                    after[n]()

        def scattered(k, j, lag):
            return (k - lag) % 4, ((k - lag) // 4 + j + 1) * 64

        def wait_scatter(eng, k, j, lag, before=0):
            b, count = scattered(k, j, lag)
            count = count - 64 * before
            if not isinstance(count, int) or count > 0:
                eng.wait_ge(sc_out[b], count)

        EXTRA = 4

        TURNS = BLOCKS // NX
        COMBINE = TURNS - UNITS // HALVES // 2

        def experts(eng, step, along=None, early=None, midway=None):
            for k in range(NX):
                step(0, k)
            if early is not None:
                early()
            for turns in ((1, TURNS // HALVES), (TURNS // HALVES, COMBINE)):
                with eng.Fori(*turns) as j:
                    for k in range(NX):
                        step(j, k)
                if midway is not None and turns[0] == 1:
                    midway()

            def turn(j):
                for k in range(NX):
                    step(j, k)
                    if along is not None and NX - 2 <= k:
                        along(j, k - (NX - 2))

            turn(COMBINE)
            with eng.Fori(COMBINE + 1, TURNS) as j:
                turn(j)
            for k in range(EXTRA):
                step(TURNS, k)

        def write_tails(eng, regs, h, e):
            eng.load(regs, ends[0:1, h, bass.ds(e, TAILS)])
            for i in range(TAILS):
                at = eng.snap(regs[i], min_val=0, max_val=EXPERTS * CAP - P)
                eng.dma_start(rows_in[h][bass.ds(at, P), :], zrow[:, i, :]).then_inc(tails_out[h], 16)

        x_tiles = x.rearrange("(t b) s d -> (b s) t d", b=2)
        adj_tiles = adj.rearrange("(t b) s k -> (b s) t k", b=2)
        out_tiles = out.rearrange("(t b) s d -> (b s) t d", b=2)

        results_tiles = results[0:2 * TOKENS, :].rearrange("(t p c) d -> p t (c d)", p=P, c=2)

        def q_view(t, c):
            return t[:, c, :].rearrange("p (b y) -> p b y", y=P)[:, :, 0:SQ]

        def by_board(ap):
            return ap.rearrange("p (b y) -> p b y", y=SQ)

        block = ctx.enter_context(nc.Block())

        @block.sync
        def _(sp):
            def load_x(u):
                if live(u):
                    wait(sp, "x_in", 16 * u)
                    sp.dma_start(x_all[:, bass.ds(2 * u, 2), :],
                                 x_tiles[:, bass.ds(2 * u, 2), :]).then_inc(s["x_in"], 16)

            load_x(0)
            for dst, src in ((wqkv_stage, wqkv), (wo_stage, wo), (bias_sb[:], bqkv), (eye[:], c_eye),
                             (others[:], c_others), (static_stage, c_static),
                             (bo_sb[:], bo.rearrange("(a d) -> a d", a=1).broadcast_to([P, D])),
                             (adj_sb[:], adj_tiles), (sel_sb[:], sel), (before_stage, c_before),
                             (iota[:], c_iota)):
                sp.dma_start(dst, src).then_inc(s["consts_in"], 16)

            def step(n, k, j_):
                u = n
                if live(u):
                    wait(sp, "init_pool", 1)
                    wait(sp, "kh_ready", u + 1)
                    wait(sp, "kl_ready", u + 1)
                    for j in range(4):
                        r = slice(HD * j, HD * j + HD)
                        for c in range(FC):
                            sp.dma_start(kbd[r, :, c, j, :].bitcast(F32), k_hl[r, :, c, :].bitcast(F32))\
                              .then_inc(s["kbd_in"], 16)
                load_x(n + 3)
                if live(n - 3):
                    b = (k - 3) % 4
                    wait(sp, "xn2_ready", n - 2)
                    sp.dma_start(xrow[:, b, 1, :, 0:D], xrow[:, b, 0, :, 0:D]).then_inc(row_copy[b], 16)

            def load_values():
                wait(sp, "scores0", UNITS)
                wait(sp, "scores1", UNITS)
                sp.dma_start(values_sb[:], values).then_inc(s["values_in"], 16)

            pipeline(sp, step, range(-2, UNITS + 3), {UNITS: load_values})

            def store_table(h):
                sp.wait_ge(s["tab_ready"], 2 * h + 2)
                for kind in range(2):
                    part = block_tab[kind, h * HALF_BLOCKS:(h + 1) * HALF_BLOCKS]
                    sp.dma_start(part.rearrange("(p a) -> p a", a=1), tab[0:HALF_BLOCKS, kind, h:h + 1])\
                      .then_inc(s["tab_out"], 16)

            def load_table(h):
                sp.wait_ge(s["tab_out"], 32 * (h + 1))
                part = slice(h * HALF_BLOCKS, (h + 1) * HALF_BLOCKS)
                sp.dma_start(expert_of[:, AHEAD + part.start:AHEAD + part.stop], block_tab[0:1, part])\
                  .then_inc(s["tab_in"], 16)
                sp.dma_start(start_of[:, part], block_tab[1:2, part]).then_inc(s["tab_in"], 16)

            regs = [sp.alloc_register(f"row{e}") for e in range(NX)]

            store_table(0)
            sp.wait_ge(s["zrow_ready"], 2)
            write_tails(sp, regs, 0, 0)
            load_table(0)
            write_tails(sp, regs, 0, TAILS)

            for b in range(0, 4, HALVES):
                sp.wait_ge(sc_out[b], 64 * (UNITS // 4))
            sp.wait_ge(s["spares_out"], 32)
            sp.wait_ge(tails_out[0], 16 * EXPERTS)
            sp.wait_ge(s["tab_in"], 32)
            sp.wait_ge(s["slot_ready"], UNITS)

            def load_rows(h, j, k):
                at = sp.snap(regs[k], min_val=0, max_val=ROWS - P)
                sp.dma_start(xg[:, k, :], rows_in[h][bass.ds(at, P), :]).then_inc(xg_in[k], 16)

            def next_rows(h, j):
                sp.load(regs, start_of[0:1, bass.ds(j * NX, NX)])
                for k in range(NX):
                    sp.wait_ge(s_e["xgt_done"], (j - 1) * NX + k + 1)
                    sp.wait_ge(s_e["meta_ready"], (j - 1) * NX + k + 1)
                    load_rows(h, j, k)

            def load_results(unit, buf):
                sp.dma_start(ga[:, buf], results_tiles[:, bass.ds(unit * 2, 2), :])\
                  .then_inc(ga_in[buf], 16)

            sp.load(regs, start_of[0:1, 0:NX])
            for k in range(NX):
                load_rows(0, 0, k)
            next_rows(0, 1)
            store_table(1)
            next_rows(0, 2)
            load_table(1)
            with sp.Fori(3, 3 + EXPERTS // TAILS) as j:
                next_rows(0, j)
                write_tails(sp, regs, 1, (j - 3) * TAILS)
            with sp.Fori(3 + EXPERTS // TAILS, TURNS // HALVES) as j:
                next_rows(0, j)
            for b in range(1, 4, HALVES):
                sp.wait_ge(sc_out[b], 64 * (UNITS // 4))
            sp.wait_ge(tails_out[1], 16 * EXPERTS)
            sp.wait_ge(s["tab_in"], 64)
            with sp.Fori(TURNS // HALVES, COMBINE) as j:
                next_rows(1, j)
            for q in range(NY):
                sp.wait_ge(yb_out[q], 16 * (HALF_BLOCKS // NY))
            for i in range(2):
                load_results(2 * i, i)
            next_rows(1, COMBINE)
            with sp.Fori(COMBINE + 1, TURNS) as j:
                for i in range(2):
                    sp.wait_ge(s_e["both_sum"], (j - COMBINE - 1) * 2 + i + 1)
                    load_results((j - COMBINE) * 4 + 2 * i, i)
                next_rows(1, j)

            for q in range(NY):
                sp.wait_ge(yb_out[q], 16 * (BLOCKS // NY))
            for i in range(NG):
                if i < 2:
                    sp.wait_ge(s_e["both_sum"], UNITS // 2 - 1 + i)
                load_results(2 * i + 1, i)
            with sp.Fori(1, UNITS // 2 // NG) as j:
                for i in range(NG):
                    sp.wait_ge(s_e["both_sum"], UNITS // 2 + (j - 1) * NG + i + 1)
                    load_results((j * NG + i) * 2 + 1, i)

        @block.tensor
        def _(pe):
            def parts3(dst, lh, ll, rh, rl, start, stop, **kw):
                pe.matmul(dst, lh, rh, start=start, stop=False, **kw)
                pe.matmul(dst, ll, rh, start=False, stop=False, **kw)
                return pe.matmul(dst, lh, rl, start=False, stop=stop, **kw)

            def scores(u, i):
                if not live(u):
                    return
                S = (S0, S1)[i]
                if i == 0:
                    wait(pe, "qh_ready", u + 1)
                    wait(pe, "ql_ready", u + 1)
                    wait(pe, "kbd_in", 128 * (u + 1))
                    wait(pe, "adj_ready", u + 1)
                if i == 0:
                    wait(pe, "va_ready", u + 1)
                    wait(pe, "vd_ready", u + 1)
                else:
                    wait(pe, "exp1", u)
                adj2 = adj_bias[:, i, None, :].broadcast_to([P, 2, SQ])
                pe.matmul(S[:, 0:384], eyeb[:], static_sb[:].rearrange("p h t -> p (h t)"),
                          start=True, stop=False, skip_group_check=True)
                pe.matmul(S[:, 384:512], eyeb[:], adj2,
                          start=False, stop=False, skip_group_check=True)
                for c in range(FC):
                    for b in range(2):
                        q0 = (2 * i + b) * P - b * SQ
                        k0 = i * P + b * SQ
                        mm = parts3(S[:, 256 * c:256 * c + 256],
                                    qz_h[:, c, q0:q0 + P], qz_l[:, c, q0:q0 + P],
                                    kbd[:, 0, c, :, k0:k0 + SQ], kbd[:, 1, c, :, k0:k0 + SQ],
                                    False, b == 1, skip_group_check=True)
                mm.then_inc(s[f"scores{i}"], 1)

            def project_qk(u, which):
                if not live(u):
                    return
                wait(pe, "wsplit", 4)
                wait(pe, "xth_ready", u + 1)
                wait(pe, "xtl_ready", u + 1)
                for w, B, done in (((1, KB, "k_done"), (0, QB, "q_done"))[which],):
                    if w == 0:
                        wait(pe, "pt1_ready", u - 1)
                    else:
                        wait(pe, "eg_ready", u - 3)
                        wait(pe, "rank_ready", u - 4)
                        wait(pe, "carry_ready", u - 4)
                    for f in range(FC):
                        col = slice(w * D + f * P, w * D + f * P + P)
                        for c in range(FC):
                            mm = parts3(B[:, 256 * f:256 * f + 256],
                                        wqkv_h[:, c, col], wqkv_l[:, c, col],
                                        xt_h[:, c, :], xt_l[:, c, :], c == 0, c == FC - 1)
                    mm.then_inc(s[done], 1)

            def project_v(u):
                if not live(u):
                    return
                wait(pe, "exp0", u)
                for i in range(2):
                    tok = slice(i * P, i * P + P)
                    for c in range(FC):
                        mm = parts3(VB[:, D * i:D * i + D], xt_h[:, c, tok], xt_l[:, c, tok],
                                    wqkv_h[:, c, 2 * D:], wqkv_l[:, c, 2 * D:],
                                    c == 0, c == FC - 1)
                mm.then_inc(s["v_done"], 1)

            def transposed(tile, done):
                for c in range(FC):
                    for i in range(2):
                        at = c * 2 * P + i * P
                        mm = pe.transpose(TRANS[:, at:at + P], tile(i, slice(c * P, c * P + P)), eye[:])
                mm.then_inc(s[done], 1)

            def probs_turned(u, i):
                if not live(u):
                    return
                wait(pe, f"norm{i}", u + 1)
                if i == 0:
                    wait(pe, "pt0_ready", u)
                    B = PTB
                else:
                    wait_last(pe, "qh_ready", u + 2)
                    wait_last(pe, "ql_ready", u + 2)
                    B = PT1B
                for j in range(4):
                    mm = pe.transpose(B[:, j * P:j * P + P], probs[:, i, j * P:j * P + P], eye[:])
                mm.then_inc(s[f"pt{i}_done"], 1)

            def attend(u, odd):
                if not live(u):
                    return
                wait(pe, "pt0_ready", u + 1)
                wait(pe, "pt1_ready", u + 1)
                wait(pe, "va_ready", u + 1)
                wait(pe, "vd_ready", u + 1)
                wait(pe, "oth_ready", u)
                wait(pe, "otl_ready", u)
                for i in range(2):
                    for j in range(4):
                        for b in range(2):
                            half_ = SQ * (j % 2)
                            col = (i * FC + j // 2) * P + b * SQ
                            mm = pe.matmul(OTB[half_:half_ + SQ, col:col + SQ],
                                           vbd[:, odd, i, b, j, :, :].rearrange("p r c -> p (r c)"),
                                           probs_t[:, i, j * P + b * SQ:j * P + b * SQ + SQ],
                                           start=True, stop=True)
                mm.then_inc(s["av_done"], 1)

            def project_out(u):
                if not live(u):
                    return
                wait(pe, "oth_ready", u + 1)
                wait(pe, "otl_ready", u + 1)
                wait(pe, "x2_ready", u)
                for i in range(2):
                    for c in range(FC):
                        mm = parts3(WOB[:, D * i:D * i + D], ot_h[:, i, c, :], ot_l[:, i, c, :],
                                    wo_h[:, c, :], wo_l[:, c, :], c == 0, False)
                    mm = pe.matmul(WOB[:, D * i:D * i + D], ones_r[:], bo_rows[:], start=False, stop=True)
                mm.then_inc(s["wo_done"], 1)

            def turn1(u):
                if live(u):
                    wait(pe, "consts_in", 16 * CONSTS)
                    wait(pe, "xn_ready", u + 1)
                    wait(pe, "x2t_ready", u - 3)
                    transposed(lambda i, f: xn[:, i, f], "xt_done")

            def turn2(u, b):
                if live(u):
                    wait(pe, "xn2_ready", u + 1)
                    wait_last(pe, "xth_ready", u + 4)
                    wait_last(pe, "xtl_ready", u + 4)
                    transposed(lambda i, f: xrow[:, b, 0, i, f], "t2_done")

            def gates(u):
                if not live(u):
                    return
                wait(pe, "x2t_ready", u + 1)
                wait_last(pe, "kh_ready", u + 4)
                wait_last(pe, "kl_ready", u + 4)
                wait(pe, "rank_ready", u - 1)
                wait(pe, "carry_ready", u - 1)
                for i in range(2):
                    for b in range(2):
                        tok = i * P + b * SQ
                        for c in range(FC):
                            mm = pe.matmul(GATEB[b * SQ:b * SQ + SQ, i * EXPERTS:(i + 1) * EXPERTS],
                                           x2t[:, c, tok:tok + SQ], sel_sb[:, c, :],
                                           start=c == 0, stop=c == FC - 1)
                mm.then_inc(s["gate_done"], 1)

            def ranks(u):
                if not live(u):
                    return
                wait(pe, "ch_ready", u + 1)
                wait_last(pe, "eg_ready", u + 2)
                wait(pe, "carry_ready", u)
                a, b, c = (slice(64 + EXPERTS * k, 96 + EXPERTS * k) for k in range(3))
                pe.matmul(GATEB[:, a], before[:], chosen[:, 0, :], start=True, stop=True)
                pe.matmul(GATEB[:, b], onesb[:], chosen[:, 0, :], start=True, stop=False)
                pe.matmul(GATEB[:, b], before[:], chosen[:, 1, :], start=False, stop=True)
                pe.matmul(GATEB[:, c], onesb[:], chosen[:, 0, :], start=True, stop=False)
                pe.matmul(GATEB[:, c], onesb[:], chosen[:, 1, :], start=False, stop=True)\
                  .then_inc(s["rank_done"], 1)

            def step(n, k, j_):
                probs_turned(n - 2, 0)
                probs_turned(n - 2, 1)
                scores(n - 1, 0)
                scores(n - 1, 1)
                project_qk(n, 0)
                project_qk(n, 1)
                attend(n - 2, k % 2)
                turn2(n - 3, (k - 3) % 4)
                project_v(n)
                turn1(n + 1)
                gates(n - 3)
                project_out(n - 2)
                ranks(n - 4)

            pe.wait_ge(s["tables"], 1)
            pe.wait_ge(s["init_dve"], 2)
            pe.wait_ge(s["init_pool"], 1)
            pipeline(pe, step)

            pe.wait_ge(s["values_in"], 16)
            pe.wait_ge(s["keys_in"], 16)
            pe.wait_ge(s["tab_in"], 32)
            pe.wait_ge(s["carry_ready"], UNITS)

            ids = [pe.alloc_register(f"expert{i}") for i in range(AHEAD + NX)]

            def expert_step(j, k):
                n = j * NX + k

                def ok(b):
                    return not isinstance(b, int) or 0 <= b < BLOCKS

                def w(name, count):
                    if not (isinstance(count, int) and count <= 0):
                        pe.wait_ge(s_e[name], count)

                def owner_of(at):
                    return pe.snap(ids[AHEAD + at], min_val=0, max_val=EXPERTS - 1)

                if k == 0:
                    pe.load(ids, expert_of[0:1, bass.ds(j * NX, AHEAD + NX)])

                if ok(n):
                    q, B = k % 2, (bank[0], bank[1])[k % 2]
                    pe.wait_ge(xg_in[k], 16 * (j + 1))
                    w("xgt_ready", n - 1)
                    for c in range(FC):
                        mm = pe.transpose(B[:, c * P:c * P + P], xg[:, k, c * P:c * P + P], eye[:])
                    mm.then_inc(s_e["xgt_done"], 1)
                if ok(n - 1):
                    q, B = (k - 1) % 2, (bank[2], bank[3])[(k - 1) % 2]
                    e = owner_of(k - 1)
                    w("xgt_ready", n)
                    w("hid_ready", n - 2)
                    for c in range(FC):
                        mm = pe.matmul(B[:, 0:HID], xgt[:, q, c, :], keys_sb[:, bass.ds(e, 1), c, :],
                                       start=c == 0, stop=c == FC - 1)
                    mm.then_inc(s_e["hid_done"], 1)
                if ok(n - 2):
                    q, B = k % 2, (bank[4], bank[5])[k % 2]
                    w("hid_ready", n - 1)
                    w("hidt_ready", n - 3)
                    pe.transpose(B[:, 0:P], hid[:, q, :], eye[:]).then_inc(s_e["hidt_done"], 1)
                if ok(n - 3):
                    q, B = (k - 1) % 2, (bank[6], bank[7])[(k - 1) % 2]
                    e = owner_of(k - 3)
                    w("hidt_ready", n - 2)
                    w("y_copied", n - 4)
                    pe.matmul(B[:, 0:D], hidt[:, q, :], values_sb[:, bass.ds(e, 1), :],
                              start=True, stop=True).then_inc(s_e["y_done"], 1)

            experts(pe, expert_step, midway=lambda: pe.wait_ge(s["tab_in"], 64))

        @block.scalar
        def _(act):
            act.wait_ge(s["consts_in"], 16 * CONSTS)
            act.wait_ge(s["scaled"], 2)
            nc.scalar.activation(wqkv_h[:], wqkv_stage, ACT.Copy).then_inc(s["wsplit"], 1)
            nc.scalar.activation(wo_h[:], wo_stage, ACT.Copy)
            nc.scalar.activation(bo_h.bitcast(F32R), bo_sb[:], ACT.Copy).then_inc(s["wsplit"], 1)

            def softmax(u, i):
                if not live(u):
                    return
                wait(act, f"max{i}", u + 1)
                wait(act, f"pt{i}_done", u)
                S = (S0, S1)[i]
                for h in range(HEADS):
                    a = nc.scalar.activation(probs[:, i, h * SQ:h * SQ + SQ], S[:, h * SQ:h * SQ + SQ],
                                             ACT.Exp, bias=nmax[:, i, h:h + 1], scale=1.0,
                                             accum_out=psum_p[:, i, h:h + 1])
                a.then_inc(s[f"exp{i}"], 1)

            def step(n, k, j_):
                odd = k % 2
                if live(n - 2):
                    wait(act, "pt0_done", n - 1)
                    nc.scalar.activation(probs_t[:, 0, :], PTB[:], ACT.Copy).then_inc(s["pt0_ready"], 1)
                softmax(n - 1, 0)
                if live(n):
                    wait(act, "k_done", n + 1)
                    wait(act, "kbd_in", 128 * n)
                    for f in range(FC):
                        a = nc.scalar.activation(k_hl[:, 0, f, :], KB[:, 256 * f:256 * f + 256],
                                                 ACT.Identity, bias=bias_sb[:, 1, f:f + 1], scale=1.0)
                    a.then_inc(s["kh_ready"], 1)
                softmax(n - 1, 1)
                if live(n - 2):
                    wait(act, "av_done", n - 1)
                    for f in range(FC):
                        src = OTB[:].rearrange("p (i f t) -> p i f t", i=2, f=FC)[:, :, f, :]
                        a = nc.scalar.activation(ot_h[:, :, f, :], src, ACT.Identity,
                                                 bias=bias_sb[:, 2, f:f + 1], scale=1.0)
                    a.then_inc(s["oth_ready"], 1)
                if live(n - 3):
                    wait(act, "t2_done", n - 2)
                    nc.scalar.activation(x2t[:].rearrange("p c t -> p (c t)"), TRANS[:], ACT.Copy)\
                        .then_inc(s["x2t_ready"], 1)
                if live(n):
                    wait(act, "q_done", n + 1)
                    for f in range(FC):
                        a = nc.scalar.activation(q_view(qz_h, f), by_board(QB[:, 256 * f:256 * f + 256]),
                                                 ACT.Identity, bias=bq_s[:, f:f + 1], scale=1.0)
                    a.then_inc(s["qh_ready"], 1)
                if live(n + 1):
                    wait(act, "xt_done", n + 2)
                    nc.scalar.activation(xt_h[:].rearrange("p c t -> p (c t)"), TRANS[:], ACT.Copy)\
                        .then_inc(s["xth_ready"], 1)
                if live(n):
                    wait(act, "v_done", n + 1)
                    src = VB[:].rearrange("p (i j r c) -> p i j r c", i=2, j=4, r=2)
                    for r in range(2):
                        a = nc.scalar.activation(vbd[SQ * r:SQ * r + SQ, odd, :, 0, :, r, :],
                                                 src[0:SQ, :, :, r, :], ACT.Copy)
                    a.then_inc(s["va_ready"], 1)
                if live(n - 3):
                    wait(act, "gate_done", n - 2)
                    wait(act, "eg1_ready", n - 3)
                    nc.scalar.activation(egate[:].rearrange("p i e -> p (i e)"), GATEB[:, 0:2 * EXPERTS],
                                         ACT.Exp, scale=-1.0).then_inc(s["eg_ready"], 1)

            act.wait_ge(s["init_pool"], 1)
            pipeline(act, step)

            act.wait_ge(s["zrow_ready"], 2)
            act.wait_ge(s["ends_ready"], 1)
            end_regs = [act.alloc_register(f"end{e}") for e in range(TAILS)]
            for e in range(2 * TAILS, EXPERTS, TAILS):
                write_tails(act, end_regs, 0, e)


            def w(name, count):
                if not (isinstance(count, int) and count <= 0):
                    act.wait_ge(s_e[name], count)

            def expert_step(j, k):
                n = j * NX + k

                def ok(b):
                    return not isinstance(b, int) or 0 <= b < BLOCKS
                if ok(n):
                    w("xgt_done", n + 1)
                    w("hid_done", n - 1)
                    nc.scalar.activation(xgt[:, k % 2, :, :].rearrange("p c t -> p (c t)"),
                                         (bank[0], bank[1])[k % 2][:, 0:2 * P], ACT.Copy)\
                        .then_inc(s_e["xgt_ready"], 1)
                if ok(n - 2):
                    w("hidt_done", n - 1)
                    w("y_done", n - 3)
                    nc.scalar.activation(hidt[:, k % 2, :], (bank[4], bank[5])[k % 2][:, 0:P], ACT.Copy)\
                        .then_inc(s_e["hidt_ready"], 1)

            def store_unit(count, unit, buf):
                act.wait_ge(s_e["y_ready"], count)
                act.dma_start(out_tiles[:, bass.ds(unit * 2, 2), :], yo[:, buf]).then_inc(yo_out[buf], 16)

            experts(act, expert_step,
                    lambda j, i: store_unit((j - COMBINE) * 2 + i + 1, (j - COMBINE) * 4 + 2 * i, i))
            with act.Fori(0, UNITS // 2 // NG) as j:
                for k in range(NG):
                    store_unit(UNITS // 2 + j * NG + k + 1, (j * NG + k) * 2 + 1, k)
            for k in range(NG):
                act.wait_ge(yo_out[k], 16 * (UNITS // 2 // NG + (UNITS // 4 if k < 2 else 0)))

        @block.vector
        def _(v):
            v.memset(ones_f[:], 1.0)
            v.memset(onesb[:], 1.0).then_inc(s["init_dve"], 1)
            v.memset(minus_half[:], -0.5)
            v.memset(bo_part[:], 1.0).then_inc(s["init_dve"], 1)
            v.wait_ge(s["consts_in"], 16 * CONSTS)
            v.wait_ge(s["init_dve"], 2)
            v.tensor_copy(ones_r[:], bo_part[:, 0:P]).then_inc(s["bo_made"], 1)
            v.tensor_scalar(round_up[:], iota[:], float(-CAP), float(P - 1), ALU.mult, ALU.add)
            v.wait_ge(s["disp_pool"], 1)
            v.tensor_scalar(sparei[:], pidx[:], SPARES - 1, None, ALU.bitwise_and)\
             .then_inc(s["spare_made"], 1)
            v.wait_ge(s["spare_made"], 1)
            v.tensor_scalar(spare[:], sparei[:], float(P), None, ALU.mult).then_inc(s["spare_made"], 1)
            for h in range(HALVES):
                v.tensor_scalar(carry[:, h, :], iota[:], float(CAP), None, ALU.mult)\
                 .then_inc(s["init_dve"], 1)
            v.tensor_scalar(wqkv_stage[:, :, 0:D], wqkv_stage[:, :, 0:D], SCALE, None, ALU.mult)\
             .then_inc(s["scaled"], 1)
            v.tensor_copy(static_sb[:], static_stage)
            v.tensor_copy(before[:], before_stage)
            v.tensor_copy(eyeb[:], eye[:]).then_inc(s["tables"], 1)
            v.tensor_scalar(bq_s[:], bias_sb[:, 0, :], SCALE, None, ALU.mult).then_inc(s["scaled"], 1)
            v.wait_ge(s["scaled"], 2)
            v.wait_ge(s["wsplit"], 2)
            v.tensor_tensor(wqkv_l[:], wqkv_stage, wqkv_h[:].bitcast(F32), ALU.subtract)\
             .then_inc(s["wsplit"], 1)
            v.tensor_tensor(wo_l[:], wo_stage, wo_h[:].bitcast(F32), ALU.subtract)\
             .then_inc(s["wsplit"], 1)
            v.wait_ge(s["bo_made"], 1)
            v.tensor_tensor(bo_part[:], bo_sb[:], bo_h, ALU.subtract)\
             .then_inc(s["bo_made"], 1)
            v.wait_ge(s["bo_made"], 2)
            v.tensor_scalar(bo_part[:], bo_part[:], eye[:, 1:2], None, ALU.mult)\
             .then_inc(s["bo_made"], 1)
            v.wait_ge(s["bo_made"], 3)
            v.scalar_tensor_tensor(bo_rows[:], bo_h, eye[:, 0:1], bo_part[:],
                                   ALU.mult, ALU.add).then_inc(s["bo_made"], 1)

            def stats(u, i_from, done):
                st = (st1, st2)[i_from // 2]
                for i in range(2):
                    ins = v.bn_stats(st[:, i, :], x_all[:, bass.ds(2 * u + i, 1), :]
                                     .rearrange("p a d -> p (a d)"))
                ins.then_inc(s[done], 1)

            def moments(n):
                a, b = live(n + 1), live(n - 3)
                if not (a or b):
                    return
                counts = []
                if live(n):
                    counts.append(("xn_ready", n + 1))
                if live(n - 4):
                    counts.append(("xn2_ready", n - 3))
                if live(n) or live(n - 4):
                    counts.append(("rstd_ready", n + 1))
                if a:
                    counts.append(("st1_ready", n + 2))
                if b:
                    counts.append(("st2_ready", n - 2))
                wait_apart(v, *counts)
                if a:
                    for i in range(2):
                        ins = v.bn_aggr(mv[:, i, :], st1[:, i, :])
                if b:
                    for i in range(2):
                        ins = v.bn_aggr(mv[:, 2 + i, :], st2[:, i, :])
                ins.then_inc(s["mv_ready"], 1)
                wait(v, "mv_ready", n + 2)
                lo, hi = (0 if a else 2), (4 if b else 2)
                v.tensor_scalar(ve[:, lo:hi], mv[:, lo:hi, 1], EPS, None, ALU.add)\
                 .then_inc(s["ve_ready"], 1)

            def split_low(done, waits, items):
                for name, count in waits:
                    wait(v, name, count)
                for dst, src, bias, high in items:
                    ins = v.scalar_tensor_tensor(dst, src, bias, high, ALU.add, ALU.subtract)
                ins.then_inc(s[done], 1)

            def normalise(dst, u, at, done):
                for i in range(2):
                    ins = v.tensor_scalar(dst(i), x_all[:, bass.ds(2 * u + i, 1), :]
                                          .rearrange("p a d -> p (a d)"),
                                          mv[:, at + i, 0:1], rstd[:, at + i:at + i + 1],
                                          ALU.subtract, ALU.mult)
                ins.then_inc(s[done], 1)

            def step(n, k, j_):
                odd = k % 2
                if live(n - 2):
                    wait(v, "pt1_done", n - 1)
                    v.tensor_copy(probs_t[:, 1, :], PT1B[:]).then_inc(s["pt1_ready"], 1)
                if live(n - 3):
                    wait_apart(v, ("x2_ready", n - 2))
                    stats(n - 3, 2, "st2_ready")
                if live(n + 1):
                    wait_apart(v, ("x_in", 16 * (n + 2)))
                    stats(n + 1, 0, "st1_ready")
                if live(n - 1):
                    maxima(n - 1, 0)
                moments(n)
                if live(n - 3):
                    wait(v, "rstd_ready", n + 2)
                    wait(v, "t2_done", n - 3)
                    wait_scatter(v, k, j_, 3, 1)
                    normalise(lambda i: xrow[:, (k - 3) % 4, 0, i, 0:D], n - 3, 2, "xn2_ready")
                if live(n - 1):
                    maxima(n - 1, 1)
                if live(n - 1):
                    reciprocals(n - 1, 0)
                if live(n):
                    split_low("kl_ready", [("kh_ready", n + 1)],
                              [(k_hl[:, 1, f, :], KB[:, 256 * f:256 * f + 256], bias_sb[:, 1, f:f + 1],
                                k_hl[:, 0, f, :].bitcast(F32)) for f in range(FC)])
                if live(n - 4):
                    route(n - 4, (k - 4) % 4)
                if live(n + 1):
                    wait(v, "rstd_ready", n + 2)
                    wait(v, "xt_done", n + 1)
                    normalise(lambda i: xn[:, i, :], n + 1, 0, "xn_ready")
                if live(n - 2):
                    src = OTB[:].rearrange("p (i f t) -> p i f t", i=2, f=FC)
                    split_low("otl_ready", [("oth_ready", n - 1)],
                              [(ot_l[:, :, f, :], src[:, :, f, :], bias_sb[:, 2, f:f + 1],
                                ot_h[:, :, f, :].bitcast(F32)) for f in range(FC)])
                if live(n):
                    wait(v, "v_done", n + 1)
                    src = VB[:].rearrange("p (i j r c) -> p i j r c", i=2, j=4, r=2)
                    for r in range(2):
                        ins = v.tensor_copy(vbd[SQ * r:SQ * r + SQ, odd, :, 1, :, r, :],
                                            src[SQ:P, :, :, r, :])
                    ins.then_inc(s["vd_ready"], 1)
                if live(n):
                    split_low("ql_ready", [("qh_ready", n + 1)],
                              [(q_view(qz_l, f), by_board(QB[:, 256 * f:256 * f + 256]),
                                bq_s[:, f:f + 1], q_view(qz_h, f).bitcast(F32)) for f in range(FC)])
                if live(n - 1):
                    reciprocals(n - 1, 1)
                if live(n + 1):
                    wait(v, "xth_ready", n + 2)
                    v.tensor_tensor(xt_l[:].rearrange("p c t -> p (c t)"), TRANS[:],
                                    xt_h[:].bitcast(F32).rearrange("p c t -> p (c t)"), ALU.subtract)\
                     .then_inc(s["xtl_ready"], 1)
                if live(n - 2):
                    wait(v, "wo_done", n - 1)
                    tiles = x_all[:, bass.ds(2 * (n - 2), 2), :]
                    v.tensor_tensor(tiles, WOB[:].rearrange("p (i d) -> p i d", i=2), tiles, ALU.add)\
                     .then_inc(s["x2_ready"], 1)
                if live(n - 4):
                    wait(v, "rank_done", n - 3)
                    wait(v, "carry_ready", n - 4)
                    wait(v, "slot_ready", n - 4)
                    v.tensor_tensor(rank_row[:],
                                    GATEB[:, 64:64 + 2 * EXPERTS].rearrange("p (i e) -> p i e", i=2),
                                    carry[:, odd, None, :].broadcast_to([P, 2, EXPERTS]), ALU.add)\
                     .then_inc(s["rank_ready"], 1)
                    wait(v, "rank_ready", n - 3)
                    v.tensor_tensor(carry[:, odd, :], GATEB[:, 128:128 + EXPERTS], carry[:, odd, :], ALU.add)\
                     .then_inc(s["carry_ready"], 1)
                    v.tensor_tensor(slots_by[:], picks[:],
                                    rank_row[:, :, None, :].broadcast_to([P, 2, 2, EXPERTS]), ALU.mult)\
                     .then_inc(s["slots_by_ready"], 1)
                    wait(v, "slots_by_ready", n - 3)
                    wait_scatter(v, k, j_, 6)
                    with nc.allow_low_precision(reason="whole numbers below 2**24, exact"):
                        v.tensor_reduce(slot[:, k % 2, :], slots_by[:].rearrange("p i c e -> p (i c) e"),
                                        AX.X, ALU.add).then_inc(s["slot_ready"], 1)

            def maxima(u, i):
                wait(v, f"scores{i}", u + 1)
                v.tensor_reduce(nmax[:, i, :], (S0, S1)[i][:].rearrange("p (h t) -> p h t", h=HEADS),
                                AX.X, ALU.max, negate=True).then_inc(s[f"max{i}"], 1)

            def reciprocals(u, i):
                wait(v, f"exp{i}", u + 1)
                wait(v, f"norm{i}", u)
                v.reciprocal(rsum[:, i, :], psum_p[:, i, :]).then_inc(s[f"rs{i}"], 1)

            def route(u, b):
                wait(v, "eg_ready", u + 1)
                wait(v, "sel_ready", u)
                v.tensor_scalar(egate1[:], egate[:], 1.0, None, ALU.add).then_inc(s["eg1_ready"], 1)
                wait(v, "eg1_ready", u + 1)
                wait(v, "topi_ready", u)
                v.reciprocal(gate[:], egate1[:]).then_inc(s["sel_ready"], 1)
                wait_apart(v, ("sel_ready", u + 1))
                for i in range(2):
                    ins = v.max(top[:, i, :], gate[:, i, :])
                ins.then_inc(s["top_ready"], 1)
                wait(v, "top_ready", u + 1)
                v.tensor_copy(xrow[:, b, :, :, GATE].rearrange("p c i -> p i c"), top[:, :, 0:2])\
                 .then_inc(s["gate_kept"], 1)
                wait_apart(v, ("topf_ready", u))
                for i in range(2):
                    ins = v.max_index(topi[:, i, :], top[:, i, :], gate[:, i, :])
                ins.then_inc(s["topi_ready"], 1)

            v.wait_ge(s["wsplit"], 4)
            count = [0]

            def link(ins):
                count[0] += 1
                ins.then_inc(s["disp"], 1)
                v.wait_ge(s["disp"], count[0])

            def dispatch(h):
                v.wait_ge(s["scores1"], UNITS)
                v.wait_ge(s["carry_ready"], UNITS + h + 1 - HALVES)
                v.tensor_copy(ends[:, h, :], carry[:, h, :]).then_inc(s["ends_ready"], 1)
                link(v.tensor_tensor(blocksi[:, 0, :], carry[:, h, :], round_up[:], ALU.add))
                link(v.tensor_scalar(blocksi[:, 1, :], blocksi[:, 0, :], 7, None, ALU.logical_shift_right))
                link(v.tensor_copy(blocksf[:], blocksi[:, 1, :]))
                link(v.tensor_tensor_scan(cum[:], ones_f[:], blocksf[:], 0.0, ALU.mult, ALU.add))
                link(v.tensor_scalar(below[:], cum[:], pidxf[:, 0:1], None, ALU.is_le))
                v.tensor_tensor(owned[:], below[:], blocksf[:], ALU.mult).then_inc(s["owned_ready"], 1)
                link(v.tensor_reduce(owner[:], below[:], AX.X, ALU.add))
                v.wait_ge(s["owned_ready"], h + 1)
                v.tensor_scalar(tab[:, 0, h:h + 1], owner[:], float(EXPERTS - 1), None, ALU.min)\
                 .then_inc(s["tab_ready"], 1)
                v.tensor_scalar(in_spares[:], owner[:], float(EXPERTS), spare[:, 0:1],
                                ALU.is_equal, ALU.mult)
                link(v.tensor_reduce(first[:], owned[:], AX.X, ALU.add))
                link(v.tensor_scalar(start[:], first[:], pidxf[:, 0:1], float(-P), ALU.subtract, ALU.mult))
                link(v.scalar_tensor_tensor(start[:], owner[:], float(CAP), start[:], ALU.mult, ALU.add))
                v.scalar_tensor_tensor(tab[:, 1, h:h + 1], start[:], float(EXPERTS * CAP), in_spares[:],
                                       ALU.min, ALU.add).then_inc(s["tab_ready"], 1)

            pipeline(v, step, after={UNITS + 2: lambda: dispatch(0)})


            def w(name, count):
                if not (isinstance(count, int) and count <= 0):
                    v.wait_ge(s_e[name], count)

            def expert_step(j, k):
                n = j * NX + k

                def ok(b):
                    return not isinstance(b, int) or 0 <= b < BLOCKS
                if ok(n):
                    v.wait_ge(xg_in[k], 16 * (j + 1))
                    if not (isinstance(j, int) and j == 0):
                        v.wait_ge(yb_out[k % NY], 16 * (j * (NX // NY) - (1 if k < NY else 0)))
                    v.tensor_copy(meta[:, k, :], xg[:, k, DEST:GATE + 1])
                    v.tensor_copy(dest[:, k:k + 1], xg[:, k, DEST:GATE]).then_inc(s_e["meta_ready"], 1)
                if ok(n - 1):
                    q = (k - 1) % 2
                    w("hid_done", n)
                    w("hidt_done", n - 2)
                    v.tensor_scalar(hid[:, q, :], (bank[2], bank[3])[q][:, 0:HID], 0.0, None, ALU.max)\
                     .then_inc(s_e["hid_ready"], 1)
                if ok(n - 3):
                    q = (k - 1) % 2
                    w("y_done", n - 2)
                    sent = j * (NX // NY) + (k - 3 - (k - 3) % NY) // NY
                    if not (isinstance(sent, int) and sent <= 0):
                        v.wait_ge(yb_out[(k - 3) % NY], 16 * sent)
                    v.tensor_scalar(yb[:, (k - 3) % NY, :], (bank[6], bank[7])[q][:, 0:D],
                                    meta[:, (k - 3) % NX, 1:2], None, ALU.mult)\
                     .then_inc(s_e["y_copied"], 1)

            def combine(order, unit, buf, use):
                v.wait_ge(ga_in[buf], 16 * (use + 1))
                if not (isinstance(use, int) and use == 0):
                    v.wait_ge(yo_out[buf], 16 * use)
                v.tensor_tensor(yo[:, buf], ga[:, buf, :, 0, :], ga[:, buf, :, 1, :], ALU.add)\
                 .then_inc(s_e["both_sum"], 1)
                v.wait_ge(s_e["both_sum"], order + 1)
                v.tensor_tensor(yo[:, buf], yo[:, buf], x_all[:, bass.ds(2 * unit, 2), :], ALU.add)\
                 .then_inc(s_e["y_ready"], 1)

            experts(v, expert_step, early=lambda: dispatch(1), along=
                    lambda j, i: combine((j - COMBINE) * 2 + i, (j - COMBINE) * 4 + 2 * i, i, j - COMBINE))

            def combine_odd(j, k):
                combine(UNITS // 2 + j * NG + k, (j * NG + k) * 2 + 1, k, j + (UNITS // 4 if k < 2 else 0))

            for k in range(NG):
                combine_odd(0, k)
            with v.Fori(1, UNITS // 2 // NG) as j:
                for k in range(NG):
                    combine_odd(j, k)

        @block.gpsimd
        def _(pool):
            g = nc.gpsimd
            for t in (kbd, qz_h, qz_l):
                g.memset(t[:].bitcast(F32), 0.0)
            g.memset(vbd[:], 0.0)
            g.memset(expert_of[:], 0)
            g.iota(pidx[:], pattern=[[1, 1]], base=0, channel_multiplier=1).then_inc(s["init_pool"], 1)
            pool.wait_ge(s["init_pool"], 1)
            g.tensor_copy(pidxf[:], pidx[:]).then_inc(s["disp_pool"], 1)
            g.iota(place[:, 0:16], pattern=[[4 * P, 4], [1, 2], [2 * P, 2]], base=0, channel_multiplier=2)
            g.iota(place[:, 16:], pattern=[[P, SPARES + TAILS]], base=2 * TOKENS, channel_multiplier=1)
            g.memset(zrow[:], 0.0).then_inc(s["disp_pool"], 1)
            pool.wait_ge(s["disp_pool"], 2)
            g.tensor_copy(xrow[:, :, :, :, DEST],
                          place[:, 0:16].rearrange("p (b c i) -> p b c i", b=4, c=2))
            g.tensor_copy(zrow[:, 0:SPARES, DEST], place[:, 16:16 + SPARES]).then_inc(s["zrow_ready"], 1)
            pool.wait_ge(s["zrow_ready"], 1)
            for h in range(HALVES):
                pool.dma_start(rows_in[h][EXPERTS * CAP:, :].rearrange("(b p) d -> p b d", p=P), zrow[:, 0:SPARES, :])\
                    .then_inc(s["spares_out"], 16)
            pool.wait_ge(s["wsplit"], 4)
            pool.wait_ge(s["bo_made"], 4)
            pool.dma_start(keys_sb[:], keys).then_inc(s["keys_in"], 16)
            pool.wait_ge(s["spares_out"], 16 * HALVES)
            g.tensor_copy(zrow[:, :, DEST], place[:, 16 + SPARES:]).then_inc(s["zrow_ready"], 1)
            pool.wait_ge(s["consts_in"], 16 * CONSTS)

            def deviations(n):
                a, b = live(n + 1), live(n - 3)
                if not (a or b):
                    return
                lo, hi = (0 if a else 2), (4 if b else 2)
                wait(pool, "ve_ready", n + 2)
                wait_last(pool, "xn_ready", n + 1)
                wait(pool, "xn2_ready", n - 3)
                wait_last(pool, "topi_ready", n - 4)
                g.tensor_tensor(rstd[:, lo:hi], ve[:, lo:hi], minus_half[:, lo:hi], ALU.pow)\
                 .then_inc(s["rstd_ready"], 1)

            def step(n, k, j_):
                deviations(n)
                if live(n - 4):
                    next_places(k, j_)
                if live(n):
                    u = n
                    others2 = others[:, None, :].broadcast_to([P, 2, SQ])
                    wait_apart(pool, ("adj_ready", u))
                    g.tensor_copy(adj_f[:], adj_sb[:, bass.ds(2 * u, 2), :]).then_inc(s["adj_cast"], 1)
                    wait(pool, "adj_cast", u + 1)
                    g.tensor_tensor(adj_f[:], adj_f[:], others2, ALU.mult).then_inc(s["adj_part"], 1)
                    wait(pool, "adj_part", u + 1)
                    wait(pool, "scores1", u)
                    g.tensor_tensor(adj_bias[:], others2, adj_f[:], ALU.subtract)\
                     .then_inc(s["adj_ready"], 1)
                if live(n - 5):
                    scatter(n - 5, k, j_, 0)
                if live(n - 1):
                    normalise_probs(n - 1, 0)
                if live(n - 4):
                    picks_of(n - 4)
                if live(n - 1):
                    normalise_probs(n - 1, 1)
                if live(n - 5):
                    scatter(n - 5, k, j_, 1)

            def next_places(k, j_):
                b, count = scattered(k, j_, 4)
                if isinstance(count, int):
                    if count <= 64:
                        return
                    gone = count - 64
                else:
                    gone = pool.to_reg(count - 64)
                pool.wait_ge(s["consts_in"], 16 * CONSTS)
                pool.wait_ge(sc_out[b], gone)
                g.tensor_scalar(xrow[:, b, :, :, DEST], xrow[:, b, :, :, DEST], float(16 * P), None,
                                ALU.add)

            def scatter(u, k, j_, i):
                b, count = scattered(k, j_, 5)
                copied = 16 * ((k - 5) // 4 + j_ + 1)
                if not isinstance(copied, int):
                    copied = pool.to_reg(copied)
                wait_apart(pool, ("slot_ready", u + 1), ("gate_kept", u + 1))
                pool.wait_ge(row_copy[b], copied)
                for c in range(2):
                    at = slot[:, (k - 5) % 2, 2 * i + c:2 * i + c + 1]
                    pool.indirect_dma_start(rows_in[(k - 5) % 2], bass.IndirectOffsetOnAxis(ap=at, axis=0),
                                            xrow[:, b, c, i, :], None).then_inc(sc_out[b], 16)

            def normalise_probs(u, i):
                wait(pool, f"rs{i}", u + 1)
                pr = probs[:, i, :].rearrange("p (h t) -> p h t", h=HEADS)
                g.tensor_tensor(pr, pr, rsum[:, i, :, None].broadcast_to([P, HEADS, SQ]), ALU.mult)\
                 .then_inc(s[f"norm{i}"], 1)

            def picks_of(u):
                wait_apart(pool, ("topi_ready", u + 1))
                g.tensor_copy(topf[:], topi[:, :, 0:2]).then_inc(s["topf_ready"], 1)
                wait_apart(pool, ("topf_ready", u + 1), ("ch_ready", u), ("slots_by_ready", u))
                for i in range(2):
                    for c in range(2):
                        ins = g.tensor_scalar(picks[:, i, c, :], iota[:], topf[:, i, c:c + 1], None,
                                              ALU.is_equal)
                ins.then_inc(s["oh_ready"], 1)
                wait(pool, "oh_ready", u + 1)
                wait(pool, "rank_done", u)
                g.tensor_tensor(chosen[:], picks[:, :, 0, :], picks[:, :, 1, :], ALU.add)\
                 .then_inc(s["ch_ready"], 1)

            pipeline(pool, step)

            def send(j, k):
                copied = pool.to_reg(j * NX + k + 1)
                pool.wait_ge(s["consts_in"], 16 * CONSTS)
                pool.wait_ge(s_e["y_copied"], copied)
                pool.indirect_dma_start(
                    results, bass.IndirectOffsetOnAxis(ap=dest[:, k:k + 1], axis=0),
                    yb[:, k % NY, :], None).then_inc(yb_out[k % NY], 16)

            with pool.Fori(0, BLOCKS // NX) as j:
                for k in range(NX):
                    send(j, k)


def kernel(**inputs):
    import numpy as np
    import concourse.bacc as bacc
    from concourse.bass_utils import run_bass_kernel_spmd

    def chunks(a):
        return np.ascontiguousarray(a.reshape(FC, P, -1).transpose(1, 0, 2))

    a = {k: np.asarray(v) for k, v in inputs.items()}
    arrays = {
        "x": a["x"],
        "adj": a["adj"],
        "wqkv": chunks(np.concatenate([a["L0_gnn_Wq"].T, a["L0_gnn_Wk"].T, a["L0_gnn_Wv"].T], axis=1)),
        "wo": chunks(a["L0_gnn_Wo"].T),
        "bqkv": np.ascontiguousarray(np.stack([a["L0_gnn_bq"], a["L0_gnn_bk"], a["L0_gnn_bv"]])
                                     .reshape(3, FC, P).transpose(2, 0, 1)),
        "bo": a["L0_gnn_bo"],
        "sel": chunks(a["L0_ffn_expert_sel"].T),
        "keys": np.ascontiguousarray(a["L0_ffn_keys"].reshape(EXPERTS, FC, P, HID).transpose(2, 0, 1, 3)),
        "values": np.ascontiguousarray(a["L0_ffn_values"].transpose(1, 0, 2)),
        **constants(),
    }
    nc = bacc.Bacc("TRN2", target_bir_lowering=False, num_devices=1)
    args = {k: nc.dram_tensor(f"in_{k}", v.shape, mybir.dt.from_np(v.dtype), kind="ExternalInput").ap()
            for k, v in arrays.items()}
    out = nc.dram_tensor("out_y", (BOARDS, SQ, D), F32, kind="ExternalOutput").ap()
    build(nc, out=out, **args)
    r = run_bass_kernel_spmd(nc, [{f"in_{k}": v for k, v in arrays.items()}], core_ids=[0])
    return r.results[0]["out_y"]
```

```python
from contextlib import ExitStack

import concourse.bass as bass
from concourse import mybir

F32 = mybir.dt.float32
F32R = mybir.dt.float32r
BF16 = mybir.dt.bfloat16
I32 = mybir.dt.int32
U32 = mybir.dt.uint32
U8 = mybir.dt.uint8
ALU = mybir.AluOpType
ACT = mybir.ActivationFunctionType
AX = mybir.AxisListType

P = 128
BOARDS, SQ, D = 128, 64, 256
HEADS = 8
HD = D // HEADS
EXPERTS, HID = 32, 128
TOKENS = BOARDS * SQ
TILES = TOKENS // P
UNITS = TILES // 2
FC = D // P
SCALE = HD ** -0.5
EPS = 1e-5
MASKED = -1e9
HALVES = 2
HALF_BLOCKS = 2 * TOKENS // HALVES // P + EXPERTS
BLOCKS = HALVES * HALF_BLOCKS
CAP = TOKENS // HALVES + P
SPARES = 4
ROWS = EXPERTS * CAP + SPARES * P
ROW = D + 2
DEST, GATE = D, D + 1
TAILS = 8
RESULTS = 2 * TOKENS + (SPARES + TAILS) * P
QPAD = 4 * P


def static_masks():
    import numpy as np
    sq = np.arange(SQ)
    r, f = sq // 8, sq % 8
    ri, rj, fi, fj = r[:, None], r[None, :], f[:, None], f[None, :]
    dr, df = np.abs(ri - rj), np.abs(fi - fj)
    eye = np.eye(SQ, dtype=bool)
    masks = [fi == fj, ri == rj, ri - fi == rj - fj, ri + fi == rj + fj,
             ((dr == 2) & (df == 1)) | ((dr == 1) & (df == 2)) | eye, (dr <= 1) & (df <= 1)]
    bias = np.where(np.stack(masks, 1), 0.0, MASKED)
    return np.concatenate([bias, bias]).astype(np.float32)


def constants():
    import numpy as np
    eye = np.eye(P, dtype=np.float32)
    return {
        "c_static": static_masks(),
        "c_eye": eye,
        "c_others": np.concatenate([np.where(np.eye(SQ), 0, MASKED).astype(np.float32)] * 2),
        "c_before": np.triu(np.ones((P, P), np.float32), 1),
        "c_iota": np.tile(np.arange(EXPERTS, dtype=np.float32), (P, 1)),
    }


def build(nc, x, adj, wqkv, wo, bqkv, bo, sel, keys, values, c_static, c_eye, c_others,
          c_before, c_iota, out):
    ctx = ExitStack()
    with ctx:
        def sb(name, shape, dt, where=ctx):
            return where.enter_context(nc.sbuf_tensor(name, shape, dt))

        def sem(name):
            return ctx.enter_context(nc.semaphore(name))

        rows_in = [nc.dram_tensor(f"rows_in{h}", (ROWS, ROW), F32).ap() for h in range(HALVES)]
        results = nc.dram_tensor("results", (RESULTS, D), F32).ap()
        block_tab = nc.dram_tensor("block_tab", (2, BLOCKS), I32).ap()

        x_all = sb("x_all", [P, TILES, D], F32)
        keys_sb = sb("keys_sb", [P, EXPERTS, FC, HID], F32)
        adj_sb = sb("adj_sb", [P, TILES, SQ], U8)
        static_sb = sb("static_sb", [P, 6, SQ], BF16)
        eye = sb("eye", [P, P], F32)
        eyeb = sb("eyeb", [P, P], BF16)
        before = sb("before", [P, P], BF16)
        onesb = sb("onesb", [P, P], BF16)
        iota = sb("iota", [P, EXPERTS], F32)
        round_up = sb("round_up", [P, EXPERTS], F32)
        warm = sb("warm", [P, 1], F32)
        ones_f = sb("ones_f", [P, EXPERTS], F32)
        sparei = sb("sparei", [P, 1], I32)
        spare = sb("spare", [P, 1], F32)
        pidx = sb("pidx", [P, 1], I32)
        pidxf = sb("pidxf", [P, 1], F32)
        zrow = sb("zrow", [P, TAILS, ROW], F32)
        xrow = sb("xrow", [P, 4, 2, 2, ROW], F32)
        slot = sb("slot", [P, 2, 4], I32)
        carry = sb("carry", [P, HALVES, EXPERTS], F32)
        place = sb("place", [P, 16 + SPARES + TAILS], I32)
        ends = sb("ends", [P, HALVES, EXPERTS], I32)
        AHEAD = 4
        blocksi = sb("blocksi", [P, 2, EXPERTS], I32)
        blocksf = sb("blocksf", [P, EXPERTS], F32)
        cum = sb("cum", [P, EXPERTS], F32)
        below = sb("below", [P, EXPERTS], F32)
        owned = sb("owned", [P, EXPERTS], F32)
        owner = sb("owner", [P, 1], F32)
        first = sb("first", [P, 1], F32)
        start = sb("start", [P, 1], F32)
        in_spares = sb("in_spares", [P, 1], F32)
        tab = sb("tab", [P, 2, HALVES], I32)
        start_of = sb("start_of", [1, BLOCKS], I32)
        expert_of = sb("expert_of", [1, AHEAD + BLOCKS + 8], I32)

        early = ExitStack()
        wqkv_h = sb("wqkv_h", [P, FC, 3 * D], F32R, early)
        wqkv_l = sb("wqkv_l", [P, FC, 3 * D], F32R, early)
        kbd = sb("kbd", [P, 2, FC, 4, 2 * P], F32R, early)
        qz_h = sb("qz_h", [P, FC, QPAD], F32R, early)
        qz_l = sb("qz_l", [P, FC, QPAD], F32R, early)
        k_hl = sb("k_hl", [P, 2, FC, 2 * P], F32R, early)
        xt_h = sb("xt_h", [P, FC, 2 * P], F32R, early)
        xt_l = sb("xt_l", [P, FC, 2 * P], F32R, early)
        wo_h = sb("wo_h", [P, FC, D], F32R, early)
        wo_l = sb("wo_l", [P, FC, D], F32R, early)
        vbd = sb("vbd", [P, 2, 2, 2, 4, 2, HD], F32, early)
        probs = sb("probs", [P, 2, 512], F32, early)
        probs_t = sb("probs_t", [P, 2, 512], F32, early)
        ot_h = sb("ot_h", [P, 2, FC, P], F32R, early)
        ot_l = sb("ot_l", [P, 2, FC, P], F32R, early)
        xn = sb("xn", [P, 2, D], F32, early)
        ones_r = sb("ones_r", [P, P], F32R, early)
        bo_rows = sb("bo_rows", [P, D], F32R, early)
        rank_row = sb("rank_row", [P, 2, EXPERTS], F32, early)
        slots_by = sb("slots_by", [P, 2, 2, EXPERTS], F32, early)
        x2t = sb("x2t", [P, FC, 2 * P], F32, early)
        sel_sb = sb("sel_sb", [P, FC, EXPERTS], F32, early)
        bias_sb = sb("bias_sb", [P, 3, FC], F32, early)
        bq_s = sb("bq_s", [P, FC], F32, early)
        others = sb("others", [P, SQ], F32, early)
        adj_f = sb("adj_f", [P, 2, SQ], F32, early)
        adj_bias = sb("adj_bias", [P, 2, SQ], BF16, early)
        st1 = sb("st1", [P, 2, 6], F32, early)
        st2 = sb("st2", [P, 2, 6], F32, early)
        mv = sb("mv", [P, 4, 2], F32, early)
        ve = sb("ve", [P, 4], F32, early)
        minus_half = sb("minus_half", [P, 4], F32, early)
        rstd = sb("rstd", [P, 4], F32, early)
        nmax = sb("nmax", [P, 2, HEADS], F32, early)
        psum_p = sb("psum_p", [P, 2, HEADS], F32, early)
        rsum = sb("rsum", [P, 2, HEADS], F32, early)
        egate = sb("egate", [P, 2, EXPERTS], F32, early)
        egate1 = sb("egate1", [P, 2, EXPERTS], F32, early)
        gate = sb("gate", [P, 2, EXPERTS], F32, early)
        top = sb("top", [P, 2, 8], F32, early)
        topi = sb("topi", [P, 2, 8], U32, early)
        topf = sb("topf", [P, 2, 2], F32, early)
        picks = sb("picks", [P, 2, 2, EXPERTS], BF16, early)
        chosen = sb("chosen", [P, 2, EXPERTS], BF16, early)
        early.close()
        values_sb = sb("values_sb", [P, EXPERTS, D], F32)
        NX = 8
        NY = 4
        xg = sb("xg", [P, NX, ROW], F32)
        meta = sb("meta", [P, NX, 2], F32)
        dest = sb("dest", [P, NX], I32)
        xgt = sb("xgt", [P, 2, FC, P], F32)
        hid = sb("hid", [P, 2, P], F32)
        block_keys = sb("block_keys", [P, 2, FC, HID], F32)
        yb = sb("yb", [P, NY, D], F32)
        NG = 4
        ga = sb("ga", [P, NG, 2, 2, D], F32)
        yo = sb("yo", [P, NG, 2, D], F32)

        bank = [ctx.enter_context(nc.psum_tensor(f"bank{i}", [P, 512], F32)) for i in range(8)]
        TRANS, QB, KB, WOB, S0, S1, PTB, OTB = bank
        VB, PT1B, GATEB = S0, QB, KB

        names = ("x_in weights_in consts_in tables wsplit scaled "
                 "st1_ready st2_ready mv_ready ve_ready "
                 "rstd_ready xn_ready xn2_ready adj_cast adj_part adj_ready "
                 "xt_done xth_ready xtl_ready q_done k_done qh_ready ql_ready kh_ready kl_ready "
                 "kbd_in v_done va_ready vd_ready scores0 scores1 max0 max1 exp0 exp1 rs0 rs1 "
                 "norm0 norm1 pt0_done pt1_done pt0_ready pt1_ready av_done oth_ready otl_ready "
                 "wo_done x2_ready t2_done x2t_ready gate_done eg_ready eg1_ready sel_ready "
                 "top_ready topi_ready topf_ready oh_ready ch_ready rank_done rank_ready carry_ready "
                 "init_dve init_pool spare_made bo_made zrow_ready spares_out keys_in values_in "
                 "disp disp_pool owned_ready ends_ready tab_ready tab_out tab_in slots_by_ready slot_ready "
                 "gate_kept").split()
        s = {n: sem(n) for n in names}
        sc_out = [sem(f"sc_out{i}") for i in range(4)]
        s_e = {n: sem("e_" + n) for n in ("xgt_done xgt_ready key_ready hid_done hid_ready "
                                           "y_done y_copied meta_ready both_sum y_ready").split()}
        row_copy = [sem(f"row_copy{i}") for i in range(4)]
        tails_out = [sem(f"tails_out{h}") for h in range(HALVES)]
        xg_in = [sem(f"xg_in{i}") for i in range(NX)]
        yb_out = [sem(f"yb_out{i}") for i in range(NY)]
        ga_in = [sem(f"ga_in{i}") for i in range(NG)]
        yo_out = [sem(f"yo_out{i}") for i in range(NG)]
        WEIGHTS, CONSTS, KEY_LOADS = 5, 6, 8
        keys_flat = keys_sb[:].rearrange("p e c h -> p (e c h)")
        wqkv_stage = keys_flat[:, 0:FC * 3 * D].rearrange("p (c n) -> p c n", c=FC)
        wo_stage = keys_flat[:, FC * 3 * D:FC * 4 * D].rearrange("p (c n) -> p c n", c=FC)
        static_stage = keys_flat[:, 2048:2048 + 6 * SQ].rearrange("p (h t) -> p h t", h=6)
        before_stage = keys_flat[:, 3072:3072 + P]
        bo_sb, bo_h, bo_part = (keys_flat[:, 4096 + i * D:4096 + (i + 1) * D] for i in range(3))

        def wait(eng, name, count):
            if isinstance(count, int):
                if count > 0:
                    eng.wait_ge(s[name], count)
            else:
                eng.wait_ge(s[name], count)

        def wait_last(eng, name, count):
            wait(eng, name, min(count, UNITS) if isinstance(count, int) else count)

        def wait_apart(eng, *counts):
            counts = [(name, c if isinstance(c, int) else eng.snap(c)) for name, c in counts]
            eng.wait_ge(s["init_dve"], 2)
            for name, c in counts:
                wait(eng, name, c)

        def live(u):
            return not isinstance(u, int) or 0 <= u < UNITS

        FIRST, LAST = 8, UNITS - 5

        def pipeline(eng, step, rounds=range(-3, UNITS + 5), after=None):
            for n in range(rounds[0], FIRST):
                step(n, n % 4, n // 4)
                if after and n in after:
                    after[n]()
            with eng.Fori(FIRST // 4, (LAST + 1) // 4) as j:
                for k in range(4):
                    step(j * 4 + k, k, j)
            for n in range(LAST + 1, rounds[-1] + 1):
                step(n, n % 4, n // 4)
                if after and n in after:
                    after[n]()

        def scattered(k, j, lag):
            return (k - lag) % 4, ((k - lag) // 4 + j + 1) * 64

        def wait_scatter(eng, k, j, lag, before=0):
            b, count = scattered(k, j, lag)
            count = count - 64 * before
            if not isinstance(count, int) or count > 0:
                eng.wait_ge(sc_out[b], count)

        EXTRA = 2
        TURNS = BLOCKS // NX
        COMBINE = TURNS - UNITS // HALVES // 2

        def experts(eng, step, along=None, midway=None):
            for k in range(NX):
                step(0, k)
            for turns in ((1, TURNS // HALVES), (TURNS // HALVES, COMBINE)):
                with eng.Fori(*turns) as j:
                    for k in range(NX):
                        step(j, k)
                if midway is not None and turns[0] == 1:
                    midway()

            def turn(j):
                for k in range(NX):
                    step(j, k)
                    if along is not None and k in (1, 2, 4, 5):
                        along(j, (1, 2, 4, 5).index(k))

            turn(COMBINE)
            with eng.Fori(COMBINE + 1, TURNS - 1) as j:
                turn(j)
            turn(TURNS - 1)
            for k in range(EXTRA):
                step(TURNS, k)

        def store_unit(eng, unit, buf):
            eng.dma_start(out_tiles[:, bass.ds(unit * 2, 2), :], yo[:, buf]).then_inc(yo_out[buf], 16)

        def half_of(u, k):
            if isinstance(u, int) and u >= UNITS - 8:
                return (u - (UNITS - 8)) // 4
            return k % 4 // 2

        def first_half(turn, i):
            turn = turn - COMBINE
            if isinstance(turn, int) and turn == UNITS // 4 - 1:
                return UNITS - 6 + i
            return turn * 4 + i

        def second_half(j, k):
            if isinstance(j, int) and j == UNITS // 8 - 1:
                return UNITS - 4 + k
            return j * 8 + k // 2 * 4 + 2 + k % 2

        def is_block(n):
            return not isinstance(n, int) or 0 <= n < BLOCKS

        def write_tail(sp, regs, h, i):
            at = sp.snap(regs[i], min_val=0, max_val=EXPERTS * CAP - P)
            part = P // TAILS
            sp.dma_start(rows_in[h][bass.ds(at, P), :].rearrange("(p r) d -> p r d", p=part),
                         zrow[part * i:part * (i + 1), :, :]).then_inc(tails_out[h], 16)

        def write_tails(sp, regs, h, e):
            sp.load(regs, ends[0:1, h, bass.ds(e, TAILS)])
            for i in range(TAILS):
                write_tail(sp, regs, h, i)

        x_tiles = x.rearrange("(t b) s d -> (b s) t d", b=2)
        adj_tiles = adj.rearrange("(t b) s k -> (b s) t k", b=2)
        out_tiles = out.rearrange("(t b) s d -> (b s) t d", b=2)
        results_tiles = results[0:2 * TOKENS, :].rearrange("(t p c) d -> p t (c d)", p=P, c=2)

        def q_view(t, c):
            return t[:, c, :].rearrange("p (b y) -> p b y", y=P)[:, :, 0:SQ]

        def by_board(ap):
            return ap.rearrange("p (b y) -> p b y", y=SQ)

        block = ctx.enter_context(nc.Block())

        @block.sync
        def _(sp):
            def load_x(u):
                if live(u):
                    wait(sp, "x_in", 16 * u)
                    sp.dma_start(x_all[:, bass.ds(2 * u, 2), :],
                                 x_tiles[:, bass.ds(2 * u, 2), :]).then_inc(s["x_in"], 16)

            load_x(0)
            for dst, src in ((wqkv_stage, wqkv), (bias_sb[:], bqkv), (eye[:], c_eye), (wo_stage, wo),
                             (bo_sb[:], bo.rearrange("(a d) -> a d", a=1).broadcast_to([P, D]))):
                sp.dma_start(dst, src).then_inc(s["weights_in"], 16)
            load_x(1)
            for dst, src in ((others[:], c_others), (adj_sb[:], adj_tiles), (static_stage, c_static),
                             (before_stage, c_before), (iota[:], c_iota), (sel_sb[:], sel)):
                sp.dma_start(dst, src).then_inc(s["consts_in"], 16)

            def load_keys(part):
                if part == 0:
                    wait(sp, "wsplit", 4)
                    wait(sp, "bo_made", 4)
                    wait(sp, "tables", 1)
                per = EXPERTS // KEY_LOADS
                sp.dma_start(keys_sb[:, part * per:(part + 1) * per], keys[:, part * per:(part + 1) * per])\
                  .then_inc(s["keys_in"], 16)

            def step(n, k, turn):
                u = n
                if live(u):
                    wait(sp, "init_pool", 1)
                    wait(sp, "kh_ready", u + 1)
                    wait(sp, "kl_ready", u + 1)
                    for j in range(4):
                        r = slice(HD * j, HD * j + HD)
                        sp.dma_start(kbd[r, :, :, j, :].rearrange("p w c t -> p (w c) t").bitcast(F32),
                                     k_hl[r].rearrange("p w c t -> p (w c) t").bitcast(F32))\
                          .then_inc(s["kbd_in"], 16)
                load_x(n + 3)
                if live(n - 3):
                    b = (k - 3) % 4
                    wait(sp, "xn2_ready", n - 2)
                    sp.dma_start(xrow[:, b, 1, :, 0:D], xrow[:, b, 0, :, 0:D]).then_inc(row_copy[b], 16)

            def load_values(parts):
                wait(sp, "scores0", UNITS)
                wait(sp, "scores1", UNITS)
                per = EXPERTS // KEY_LOADS
                for e in range(parts[0] * per, parts[1] * per, per):
                    sp.dma_start(values_sb[:, e:e + per, :], values[:, e:e + per, :])\
                      .then_inc(s["values_in"], 16)

            def store_table(h):
                sp.wait_ge(s["tab_ready"], 2 * h + 2)
                for kind in range(2):
                    part = block_tab[kind, h * HALF_BLOCKS:(h + 1) * HALF_BLOCKS]
                    sp.dma_start(part.rearrange("(p a) -> p a", a=1), tab[0:HALF_BLOCKS, kind, h:h + 1])\
                      .then_inc(s["tab_out"], 16)

            def load_table(h):
                sp.wait_ge(s["tab_out"], 32 * (h + 1))
                part = slice(h * HALF_BLOCKS, (h + 1) * HALF_BLOCKS)
                sp.dma_start(expert_of[:, AHEAD + part.start:AHEAD + part.stop], block_tab[0:1, part])\
                  .then_inc(s["tab_in"], 16)
                sp.dma_start(start_of[:, part], block_tab[1:2, part]).then_inc(s["tab_in"], 16)

            regs = [sp.alloc_register(f"row{e}") for e in range(NX)]
            end_regs = [sp.alloc_register(f"end{e}") for e in range(TAILS)]

            def dispatch_first():
                store_table(0)
                sp.wait_ge(s["zrow_ready"], 2)
                write_tails(sp, regs, 0, 0)
                load_table(0)
                write_tails(sp, regs, 0, TAILS)

            def finish_first():
                write_tails(sp, regs, 0, 2 * TAILS)
                write_tails(sp, regs, 0, 3 * TAILS)
                load_values((0, 2))

            after = {UNITS - 1: dispatch_first, UNITS: finish_first,
                     UNITS + 1: lambda: load_values((2, 5)), UNITS + 2: lambda: load_values((5, KEY_LOADS))}
            for part in range(KEY_LOADS):
                after[part] = lambda part=part: load_keys(part)
            pipeline(sp, step, range(-1, UNITS + 3), after)

            for b in range(4):
                sp.wait_ge(sc_out[b], 64 * (UNITS // 4 - 1))
            sp.wait_ge(s["spares_out"], 32)
            sp.wait_ge(tails_out[0], 16 * EXPERTS)
            sp.wait_ge(s["tab_in"], 32)
            sp.wait_ge(s["slot_ready"], UNITS)

            def load_rows(h, j, k):
                at = sp.snap(regs[k], min_val=0, max_val=ROWS - P)
                sp.dma_start(xg[:, k, :], rows_in[h][bass.ds(at, P), :]).then_inc(xg_in[k], 16)

            def next_rows(h, j, beside=None):
                sp.load(regs, start_of[0:1, bass.ds(j * NX, NX)])
                for k in range(NX):
                    sp.wait_ge(s_e["xgt_done"], (j - 1) * NX + k + 1)
                    sp.wait_ge(s_e["meta_ready"], (j - 1) * NX + k + 1)
                    load_rows(h, j, k)
                    if beside is not None:
                        beside(k)

            def load_results(unit, buf):
                sp.dma_start(ga[:, buf], results_tiles[:, bass.ds(unit * 2, 2), :])\
                  .then_inc(ga_in[buf], 16)

            sp.load(regs, start_of[0:1, 0:NX])
            for k in range(NX):
                load_rows(0, 0, k)
            next_rows(0, 1)
            store_table(1)
            next_rows(0, 2)
            load_table(1)
            with sp.Fori(3, 3 + EXPERTS // TAILS) as j:
                sp.load(end_regs, ends[0:1, 1, bass.ds((j - 3) * TAILS, TAILS)])
                next_rows(0, j, lambda k: write_tail(sp, end_regs, 1, k))
            with sp.Fori(3 + EXPERTS // TAILS, TURNS // HALVES) as j:
                next_rows(0, j)
            for b in range(4):
                sp.wait_ge(sc_out[b], 64 * (UNITS // 4))
            sp.wait_ge(tails_out[1], 16 * EXPERTS)
            sp.wait_ge(s["tab_in"], 64)
            with sp.Fori(TURNS // HALVES, COMBINE) as j:
                next_rows(1, j)
            next_rows(1, COMBINE)
            for q in range(NY):
                sp.wait_ge(yb_out[q], 16 * (HALF_BLOCKS // NY))
            for i in range(2):
                load_results(i, i)

            def exchange(j, k):
                if k in (3, 6):
                    i = (3, 6).index(k)
                    sp.wait_ge(s_e["y_ready"], (j - COMBINE - 1) * 2 + i + 1)
                    store_unit(sp, first_half(j - 1, i), i)
                    load_results(first_half(j, i), i)

            with sp.Fori(COMBINE + 1, TURNS - 1) as j:
                next_rows(1, j, lambda k: exchange(j, k))
            next_rows(1, TURNS - 1, lambda k: exchange(TURNS - 1, k))
            for i in range(2):
                sp.wait_ge(s_e["y_ready"], (TURNS - COMBINE - 1) * 2 + i + 1)
                store_unit(sp, first_half(TURNS - 1, i), i)

            for q in range(NY):
                sp.wait_ge(yb_out[q], 16 * (BLOCKS // NY))
            for i in range(NG):
                load_results(second_half(0, i), i)

            def refill(j):
                for i in range(NG):
                    sp.wait_ge(s_e["both_sum"], UNITS // 2 + (j - 1) * NG + i + 1)
                    load_results(second_half(j, i), i)

            with sp.Fori(1, UNITS // 8 - 1) as j:
                refill(j)
            refill(UNITS // 8 - 1)

        @block.tensor
        def _(pe):
            def parts3(dst, lh, ll, rh, rl, start, stop, **kw):
                pe.matmul(dst, lh, rh, start=start, stop=False, **kw)
                pe.matmul(dst, ll, rh, start=False, stop=False, **kw)
                return pe.matmul(dst, lh, rl, start=False, stop=stop, **kw)

            def scores(u, i):
                if not live(u):
                    return
                S = (S0, S1)[i]
                if i == 0:
                    wait(pe, "qh_ready", u + 1)
                    wait(pe, "ql_ready", u + 1)
                    wait(pe, "kbd_in", 64 * (u + 1))
                    wait(pe, "adj_ready", u + 1)
                if i == 0:
                    wait(pe, "va_ready", u + 1)
                    wait(pe, "vd_ready", u + 1)
                else:
                    wait(pe, "exp1", u)
                adj2 = adj_bias[:, i, None, :].broadcast_to([P, 2, SQ])
                pe.matmul(S[:, 0:384], eyeb[:], static_sb[:].rearrange("p h t -> p (h t)"),
                          start=True, stop=False, skip_group_check=True)
                pe.matmul(S[:, 384:512], eyeb[:], adj2,
                          start=False, stop=False, skip_group_check=True)
                for c in range(FC):
                    for b in range(2):
                        q0 = (2 * i + b) * P - b * SQ
                        k0 = i * P + b * SQ
                        mm = parts3(S[:, 256 * c:256 * c + 256],
                                    qz_h[:, c, q0:q0 + P], qz_l[:, c, q0:q0 + P],
                                    kbd[:, 0, c, :, k0:k0 + SQ], kbd[:, 1, c, :, k0:k0 + SQ],
                                    False, b == 1, skip_group_check=True)
                mm.then_inc(s[f"scores{i}"], 1)

            def project_qk(u, w):
                if not live(u):
                    return
                wait(pe, "wsplit", 4)
                wait(pe, "xth_ready", u + 1)
                wait(pe, "xtl_ready", u + 1)
                if w == 0:
                    wait(pe, "pt1_ready", u - 1)
                else:
                    wait(pe, "eg_ready", u - 3)
                    wait(pe, "rank_ready", u - 4)
                    wait(pe, "carry_ready", u - 4)
                B = (QB, KB)[w]
                for f in range(FC):
                    col = slice(w * D + f * P, w * D + f * P + P)
                    for c in range(FC):
                        mm = parts3(B[:, 256 * f:256 * f + 256],
                                    wqkv_h[:, c, col], wqkv_l[:, c, col],
                                    xt_h[:, c, :], xt_l[:, c, :], c == 0, c == FC - 1)
                mm.then_inc(s[("q_done", "k_done")[w]], 1)

            def project_v(u):
                if not live(u):
                    return
                wait(pe, "exp0", u)
                for i in range(2):
                    tok = slice(i * P, i * P + P)
                    for c in range(FC):
                        mm = parts3(VB[:, D * i:D * i + D], xt_h[:, c, tok], xt_l[:, c, tok],
                                    wqkv_h[:, c, 2 * D:], wqkv_l[:, c, 2 * D:],
                                    c == 0, c == FC - 1)
                mm.then_inc(s["v_done"], 1)

            def transposed(tile, done):
                for c in range(FC):
                    for i in range(2):
                        at = c * 2 * P + i * P
                        mm = pe.transpose(TRANS[:, at:at + P], tile(i, slice(c * P, c * P + P)), eye[:])
                mm.then_inc(s[done], 1)

            def probs_turned(u, i):
                if not live(u):
                    return
                wait(pe, f"norm{i}", u + 1)
                if i == 0:
                    wait(pe, "pt0_ready", u)
                    B = PTB
                else:
                    wait_last(pe, "qh_ready", u + 2)
                    wait_last(pe, "ql_ready", u + 2)
                    B = PT1B
                for j in range(4):
                    mm = pe.transpose(B[:, j * P:j * P + P], probs[:, i, j * P:j * P + P], eye[:])
                mm.then_inc(s[f"pt{i}_done"], 1)

            def attend(u, parity):
                if not live(u):
                    return
                wait(pe, "pt0_ready", u + 1)
                wait(pe, "pt1_ready", u + 1)
                wait(pe, "va_ready", u + 1)
                wait(pe, "vd_ready", u + 1)
                wait(pe, "oth_ready", u)
                wait(pe, "otl_ready", u)
                for i in range(2):
                    for j in range(4):
                        for b in range(2):
                            half_ = SQ * (j % 2)
                            col = (i * FC + j // 2) * P + b * SQ
                            mm = pe.matmul(OTB[half_:half_ + SQ, col:col + SQ],
                                           vbd[:, parity, i, b, j, :, :].rearrange("p r c -> p (r c)"),
                                           probs_t[:, i, j * P + b * SQ:j * P + b * SQ + SQ],
                                           start=True, stop=True)
                mm.then_inc(s["av_done"], 1)

            def project_out(u):
                if not live(u):
                    return
                wait(pe, "oth_ready", u + 1)
                wait(pe, "otl_ready", u + 1)
                wait(pe, "x2_ready", u)
                for i in range(2):
                    for c in range(FC):
                        mm = parts3(WOB[:, D * i:D * i + D], ot_h[:, i, c, :], ot_l[:, i, c, :],
                                    wo_h[:, c, :], wo_l[:, c, :], c == 0, False)
                    mm = pe.matmul(WOB[:, D * i:D * i + D], ones_r[:], bo_rows[:], start=False, stop=True)
                mm.then_inc(s["wo_done"], 1)

            def turn1(u):
                if live(u):
                    wait(pe, "weights_in", 16 * WEIGHTS)
                    wait(pe, "xn_ready", u + 1)
                    wait(pe, "x2t_ready", u - 3)
                    transposed(lambda i, f: xn[:, i, f], "xt_done")

            def turn2(u, b):
                if live(u):
                    wait(pe, "xn2_ready", u + 1)
                    wait_last(pe, "xth_ready", u + 4)
                    wait_last(pe, "xtl_ready", u + 4)
                    transposed(lambda i, f: xrow[:, b, 0, i, f], "t2_done")

            def gates(u):
                if not live(u):
                    return
                wait(pe, "x2t_ready", u + 1)
                wait_last(pe, "kh_ready", u + 4)
                wait_last(pe, "kl_ready", u + 4)
                wait(pe, "rank_ready", u - 1)
                wait(pe, "carry_ready", u - 1)
                for i in range(2):
                    for b in range(2):
                        tok = i * P + b * SQ
                        for c in range(FC):
                            mm = pe.matmul(GATEB[b * SQ:b * SQ + SQ, i * EXPERTS:(i + 1) * EXPERTS],
                                           x2t[:, c, tok:tok + SQ], sel_sb[:, c, :],
                                           start=c == 0, stop=c == FC - 1)
                mm.then_inc(s["gate_done"], 1)

            def ranks(u):
                if not live(u):
                    return
                wait(pe, "ch_ready", u + 1)
                wait_last(pe, "eg_ready", u + 2)
                wait(pe, "carry_ready", u)
                a, b, c = (slice(64 + EXPERTS * k, 96 + EXPERTS * k) for k in range(3))
                pe.matmul(GATEB[:, a], before[:], chosen[:, 0, :], start=True, stop=True)
                pe.matmul(GATEB[:, b], onesb[:], chosen[:, 0, :], start=True, stop=False)
                pe.matmul(GATEB[:, b], before[:], chosen[:, 1, :], start=False, stop=True)
                pe.matmul(GATEB[:, c], onesb[:], chosen[:, 0, :], start=True, stop=False)
                pe.matmul(GATEB[:, c], onesb[:], chosen[:, 1, :], start=False, stop=True)\
                  .then_inc(s["rank_done"], 1)

            def step(n, k, turn):
                probs_turned(n - 2, 0)
                probs_turned(n - 2, 1)
                scores(n - 1, 0)
                scores(n - 1, 1)
                project_qk(n, 1)
                project_qk(n, 0)
                attend(n - 2, k % 2)
                turn2(n - 3, (k - 3) % 4)
                project_v(n)
                turn1(n + 1)
                gates(n - 3)
                project_out(n - 2)
                ranks(n - 4)

            def tables_there():
                pe.wait_ge(s["tables"], 1)
                pe.wait_ge(s["consts_in"], 16 * CONSTS)
                pe.wait_ge(s["bo_made"], 4)
                pe.wait_ge(s["init_dve"], 4)
                pe.wait_ge(s["init_pool"], 1)

            pipeline(pe, step, after={0: tables_there})

            pe.wait_ge(s["values_in"], 16 * KEY_LOADS)
            pe.wait_ge(s["tab_in"], 32)
            pe.wait_ge(s["carry_ready"], UNITS)

            ids = [pe.alloc_register(f"expert{i}") for i in range(AHEAD + NX)]

            def expert_step(j, k):
                n = j * NX + k

                def w(name, count):
                    if not (isinstance(count, int) and count <= 0):
                        pe.wait_ge(s_e[name], count)

                if k == 0:
                    pe.load(ids, expert_of[0:1, bass.ds(j * NX, AHEAD + NX)])
                if is_block(n):
                    B = (bank[0], bank[1])[k % 2]
                    pe.wait_ge(xg_in[k], 16 * (j + 1))
                    w("xgt_ready", n - 1)
                    for c in range(FC):
                        mm = pe.transpose(B[:, c * P:c * P + P], xg[:, k, c * P:c * P + P], eye[:])
                    mm.then_inc(s_e["xgt_done"], 1)
                if is_block(n - 1):
                    q, B = (k - 1) % 2, (bank[2], bank[3])[(k - 1) % 2]
                    w("xgt_ready", n)
                    w("key_ready", n)
                    w("hid_ready", n - 2)
                    for c in range(FC):
                        mm = pe.matmul(B[:, 0:P], block_keys[:, q, c, :], xgt[:, q, c, :],
                                       start=c == 0, stop=c == FC - 1)
                    mm.then_inc(s_e["hid_done"], 1)
                if is_block(n - 2):
                    q, B = k % 2, (bank[6], bank[7])[k % 2]
                    e = pe.snap(ids[AHEAD + k - 2], min_val=0, max_val=EXPERTS - 1)
                    w("hid_ready", n - 1)
                    w("y_copied", n - 3)
                    pe.matmul(B[:, 0:D], hid[:, q, :], values_sb[:, bass.ds(e, 1), :],
                              start=True, stop=True).then_inc(s_e["y_done"], 1)

            experts(pe, expert_step, midway=lambda: pe.wait_ge(s["tab_in"], 64))

        @block.scalar
        def _(act):
            act.wait_ge(s["init_dve"], 1)
            nc.scalar.activation(warm[:], ones_f[:, 0:1], ACT.Exp)
            act.wait_ge(s["weights_in"], 16 * WEIGHTS)
            act.wait_ge(s["scaled"], 2)
            nc.scalar.activation(wqkv_h[:], wqkv_stage, ACT.Copy).then_inc(s["wsplit"], 1)
            nc.scalar.activation(wo_h[:], wo_stage, ACT.Copy)
            nc.scalar.activation(bo_h.bitcast(F32R), bo_sb[:], ACT.Copy).then_inc(s["wsplit"], 1)

            def softmax(u, i):
                if not live(u):
                    return
                wait(act, f"max{i}", u + 1)
                wait(act, f"pt{i}_done", u)
                S = (S0, S1)[i]
                for h in range(HEADS):
                    a = nc.scalar.activation(probs[:, i, h * SQ:h * SQ + SQ], S[:, h * SQ:h * SQ + SQ],
                                             ACT.Exp, bias=nmax[:, i, h:h + 1], scale=1.0,
                                             accum_out=psum_p[:, i, h:h + 1])
                a.then_inc(s[f"exp{i}"], 1)

            def step(n, k, turn):
                parity = k % 2
                if live(n - 2):
                    wait(act, "pt0_done", n - 1)
                    nc.scalar.activation(probs_t[:, 0, :], PTB[:], ACT.Copy).then_inc(s["pt0_ready"], 1)
                softmax(n - 1, 0)
                if live(n):
                    wait(act, "k_done", n + 1)
                    wait(act, "kbd_in", 64 * n)
                    for f in range(FC):
                        a = nc.scalar.activation(k_hl[:, 0, f, :], KB[:, 256 * f:256 * f + 256],
                                                 ACT.Identity, bias=bias_sb[:, 1, f:f + 1], scale=1.0)
                    a.then_inc(s["kh_ready"], 1)
                softmax(n - 1, 1)
                if live(n - 2):
                    wait(act, "av_done", n - 1)
                    for f in range(FC):
                        src = OTB[:].rearrange("p (i f t) -> p i f t", i=2, f=FC)[:, :, f, :]
                        a = nc.scalar.activation(ot_h[:, :, f, :], src, ACT.Identity,
                                                 bias=bias_sb[:, 2, f:f + 1], scale=1.0)
                    a.then_inc(s["oth_ready"], 1)
                if live(n - 3):
                    wait(act, "t2_done", n - 2)
                    nc.scalar.activation(x2t[:].rearrange("p c t -> p (c t)"), TRANS[:], ACT.Copy)\
                        .then_inc(s["x2t_ready"], 1)
                if live(n + 1):
                    wait(act, "xt_done", n + 2)
                    nc.scalar.activation(xt_h[:].rearrange("p c t -> p (c t)"), TRANS[:], ACT.Copy)\
                        .then_inc(s["xth_ready"], 1)
                if live(n):
                    wait(act, "q_done", n + 1)
                    for f in range(FC):
                        a = nc.scalar.activation(q_view(qz_h, f), by_board(QB[:, 256 * f:256 * f + 256]),
                                                 ACT.Identity, bias=bq_s[:, f:f + 1], scale=1.0)
                    a.then_inc(s["qh_ready"], 1)
                if live(n - 3):
                    wait(act, "gate_done", n - 2)
                    wait(act, "eg1_ready", n - 3)
                    nc.scalar.activation(egate[:].rearrange("p i e -> p (i e)"), GATEB[:, 0:2 * EXPERTS],
                                         ACT.Exp, scale=-1.0).then_inc(s["eg_ready"], 1)
                if live(n):
                    wait(act, "v_done", n + 1)
                    src = VB[:].rearrange("p (i j r c) -> p i j r c", i=2, j=4, r=2)
                    for r in range(2):
                        a = nc.scalar.activation(vbd[SQ * r:SQ * r + SQ, parity, :, 0, :, r, :],
                                                 src[0:SQ, :, :, r, :], ACT.Copy)
                    a.then_inc(s["va_ready"], 1)

            pipeline(act, step, after={-1: lambda: act.wait_ge(s["init_pool"], 1)})

            act.wait_ge(s["keys_in"], 16 * KEY_LOADS)
            act.wait_ge(s["tab_in"], 32)
            ids = [act.alloc_register(f"expert{i}") for i in range(NX)]

            def expert_step(j, k):
                n = j * NX + k

                def w(name, count):
                    if not (isinstance(count, int) and count <= 0):
                        act.wait_ge(s_e[name], count)

                if is_block(n):
                    if k == 0:
                        act.load(ids, expert_of[0:1, bass.ds(j * NX + AHEAD, NX)])
                    e = act.snap(ids[k], min_val=0, max_val=EXPERTS - 1)
                    w("hid_done", n - 1)
                    nc.scalar.activation(block_keys[:, k % 2].rearrange("p c h -> p (c h)"),
                                         keys_sb[:, bass.ds(e, 1)].rearrange("p e c h -> p (e c h)"),
                                         ACT.Copy).then_inc(s_e["key_ready"], 1)
                    w("xgt_done", n + 1)
                    nc.scalar.activation(xgt[:, k % 2, :, :].rearrange("p c t -> p (c t)"),
                                         (bank[0], bank[1])[k % 2][:, 0:2 * P], ACT.Copy)\
                        .then_inc(s_e["xgt_ready"], 1)

            experts(act, expert_step, midway=lambda: act.wait_ge(s["tab_in"], 64))

            def store_units(j):
                for k in range(NG):
                    act.wait_ge(s_e["y_ready"], UNITS // 2 + j * NG + k + 1)
                    store_unit(act, second_half(j, k), k)

            with act.Fori(0, UNITS // 8 - 1) as j:
                store_units(j)
            store_units(UNITS // 8 - 1)
            for k in range(NG):
                act.wait_ge(yo_out[k], 16 * (UNITS // 2 // NG + (UNITS // 4 if k < 2 else 0)))

        @block.vector
        def _(v):
            v.memset(ones_f[:], 1.0)
            v.memset(onesb[:], 1.0).then_inc(s["init_dve"], 1)
            v.memset(minus_half[:], -0.5)
            v.memset(bo_part[:], 1.0).then_inc(s["init_dve"], 1)
            v.wait_ge(s["weights_in"], 16 * WEIGHTS)
            v.tensor_scalar(wqkv_stage[:, :, 0:D], wqkv_stage[:, :, 0:D], SCALE, None, ALU.mult)\
             .then_inc(s["scaled"], 1)
            v.tensor_scalar(bq_s[:], bias_sb[:, 0, :], SCALE, None, ALU.mult).then_inc(s["scaled"], 1)

            def split_weights():
                v.wait_ge(s["wsplit"], 2)
                v.wait_ge(s["scaled"], 2)
                v.tensor_tensor(wqkv_l[:], wqkv_stage, wqkv_h[:].bitcast(F32), ALU.subtract)\
                 .then_inc(s["wsplit"], 1)
                v.tensor_tensor(wo_l[:], wo_stage, wo_h[:].bitcast(F32), ALU.subtract)\
                 .then_inc(s["wsplit"], 1)
                v.wait_ge(s["consts_in"], 16 * CONSTS)
                v.tensor_copy(static_sb[:], static_stage)
                v.tensor_copy(before[:], before_stage)
                v.tensor_copy(eyeb[:], eye[:]).then_inc(s["tables"], 1)
                v.wait_ge(s["init_dve"], 2)
                v.tensor_copy(ones_r[:], bo_part[:, 0:P]).then_inc(s["bo_made"], 1)
                v.wait_ge(s["bo_made"], 1)
                v.tensor_tensor(bo_part[:], bo_sb[:], bo_h, ALU.subtract).then_inc(s["bo_made"], 1)
                v.wait_ge(s["bo_made"], 2)
                v.tensor_scalar(bo_part[:], bo_part[:], eye[:, 1:2], None, ALU.mult)\
                 .then_inc(s["bo_made"], 1)
                v.wait_ge(s["bo_made"], 3)
                v.scalar_tensor_tensor(bo_rows[:], bo_h, eye[:, 0:1], bo_part[:], ALU.mult, ALU.add)\
                 .then_inc(s["bo_made"], 1)

            def dispatch_tables():
                v.tensor_scalar(round_up[:], iota[:], float(-CAP), float(P - 1), ALU.mult, ALU.add)
                for h in range(HALVES):
                    v.tensor_scalar(carry[:, h, :], iota[:], float(CAP), None, ALU.mult)\
                     .then_inc(s["init_dve"], 1)
                v.wait_ge(s["disp_pool"], 1)
                v.tensor_scalar(sparei[:], pidx[:], SPARES - 1, None, ALU.bitwise_and)\
                 .then_inc(s["spare_made"], 1)
                v.wait_ge(s["spare_made"], 1)
                v.tensor_scalar(spare[:], sparei[:], float(P), None, ALU.mult).then_inc(s["spare_made"], 1)

            def stats(u, i_from, done):
                st = (st1, st2)[i_from // 2]
                for i in range(2):
                    ins = v.bn_stats(st[:, i, :], x_all[:, bass.ds(2 * u + i, 1), :]
                                     .rearrange("p a d -> p (a d)"))
                ins.then_inc(s[done], 1)

            def moments(n):
                a, b = live(n + 1), live(n - 3)
                if not (a or b):
                    return
                counts = []
                if live(n):
                    counts.append(("xn_ready", n + 1))
                if live(n - 4):
                    counts.append(("xn2_ready", n - 3))
                if live(n) or live(n - 4):
                    counts.append(("rstd_ready", n + 1))
                if a:
                    counts.append(("st1_ready", n + 2))
                if b:
                    counts.append(("st2_ready", n - 2))
                wait_apart(v, *counts)
                if a:
                    for i in range(2):
                        ins = v.bn_aggr(mv[:, i, :], st1[:, i, :])
                if b:
                    for i in range(2):
                        ins = v.bn_aggr(mv[:, 2 + i, :], st2[:, i, :])
                ins.then_inc(s["mv_ready"], 1)
                wait(v, "mv_ready", n + 2)
                lo, hi = (0 if a else 2), (4 if b else 2)
                v.tensor_scalar(ve[:, lo:hi], mv[:, lo:hi, 1], EPS, None, ALU.add)\
                 .then_inc(s["ve_ready"], 1)

            def split_low(done, waits, items):
                for name, count in waits:
                    wait(v, name, count)
                for dst, src, bias, high in items:
                    ins = v.scalar_tensor_tensor(dst, src, bias, high, ALU.add, ALU.subtract)
                ins.then_inc(s[done], 1)

            def normalise(dst, u, at, done):
                for i in range(2):
                    ins = v.tensor_scalar(dst(i), x_all[:, bass.ds(2 * u + i, 1), :]
                                          .rearrange("p a d -> p (a d)"),
                                          mv[:, at + i, 0:1], rstd[:, at + i:at + i + 1],
                                          ALU.subtract, ALU.mult)
                ins.then_inc(s[done], 1)

            def step(n, k, turn):
                parity = k % 2
                if live(n - 3):
                    wait_apart(v, ("x2_ready", n - 2))
                    stats(n - 3, 2, "st2_ready")
                if live(n - 1):
                    maxima(n - 1, 0)
                if live(n - 2):
                    wait(v, "pt1_done", n - 1)
                    v.tensor_copy(probs_t[:, 1, :], PT1B[:]).then_inc(s["pt1_ready"], 1)
                if live(n + 1):
                    wait_apart(v, ("x_in", 16 * (n + 2)))
                    stats(n + 1, 0, "st1_ready")
                moments(n)
                if live(n - 1):
                    maxima(n - 1, 1)
                if live(n):
                    split_low("kl_ready", [("kh_ready", n + 1)],
                              [(k_hl[:, 1, f, :], KB[:, 256 * f:256 * f + 256], bias_sb[:, 1, f:f + 1],
                                k_hl[:, 0, f, :].bitcast(F32)) for f in range(FC)])
                if live(n - 3):
                    wait(v, "rstd_ready", n + 2)
                    wait(v, "t2_done", n - 3)
                    wait_scatter(v, k, turn, 3, 1)
                    normalise(lambda i: xrow[:, (k - 3) % 4, 0, i, 0:D], n - 3, 2, "xn2_ready")
                if live(n + 1):
                    wait(v, "rstd_ready", n + 2)
                    wait(v, "xt_done", n + 1)
                    normalise(lambda i: xn[:, i, :], n + 1, 0, "xn_ready")
                if live(n - 1):
                    reciprocals(n - 1, 0)
                if live(n - 4):
                    route(n - 4, (k - 4) % 4)
                if live(n - 2):
                    src = OTB[:].rearrange("p (i f t) -> p i f t", i=2, f=FC)
                    split_low("otl_ready", [("oth_ready", n - 1)],
                              [(ot_l[:, :, f, :], src[:, :, f, :], bias_sb[:, 2, f:f + 1],
                                ot_h[:, :, f, :].bitcast(F32)) for f in range(FC)])
                if live(n):
                    wait(v, "v_done", n + 1)
                    src = VB[:].rearrange("p (i j r c) -> p i j r c", i=2, j=4, r=2)
                    for r in range(2):
                        ins = v.tensor_copy(vbd[SQ * r:SQ * r + SQ, parity, :, 1, :, r, :],
                                            src[SQ:P, :, :, r, :])
                    ins.then_inc(s["vd_ready"], 1)
                if live(n - 1):
                    reciprocals(n - 1, 1)
                if live(n + 1):
                    wait(v, "xth_ready", n + 2)
                    v.tensor_tensor(xt_l[:].rearrange("p c t -> p (c t)"), TRANS[:],
                                    xt_h[:].bitcast(F32).rearrange("p c t -> p (c t)"), ALU.subtract)\
                     .then_inc(s["xtl_ready"], 1)
                if live(n):
                    split_low("ql_ready", [("qh_ready", n + 1)],
                              [(q_view(qz_l, f), by_board(QB[:, 256 * f:256 * f + 256]),
                                bq_s[:, f:f + 1], q_view(qz_h, f).bitcast(F32)) for f in range(FC)])
                if live(n - 2):
                    wait(v, "wo_done", n - 1)
                    tiles = x_all[:, bass.ds(2 * (n - 2), 2), :]
                    v.tensor_tensor(tiles, WOB[:].rearrange("p (i d) -> p i d", i=2), tiles, ALU.add)\
                     .then_inc(s["x2_ready"], 1)
                if live(n - 4):
                    wait(v, "rank_done", n - 3)
                    wait(v, "carry_ready", n - 4)
                    wait(v, "slot_ready", n - 4)
                    own = carry[:, half_of(n - 4, k), :]
                    v.tensor_tensor(rank_row[:],
                                    GATEB[:, 64:64 + 2 * EXPERTS].rearrange("p (i e) -> p i e", i=2),
                                    own[:, None, :].broadcast_to([P, 2, EXPERTS]), ALU.add)\
                     .then_inc(s["rank_ready"], 1)
                    wait(v, "rank_ready", n - 3)
                    v.tensor_tensor(own, GATEB[:, 128:128 + EXPERTS], own, ALU.add)\
                     .then_inc(s["carry_ready"], 1)
                    v.tensor_tensor(slots_by[:], picks[:],
                                    rank_row[:, :, None, :].broadcast_to([P, 2, 2, EXPERTS]), ALU.mult)\
                     .then_inc(s["slots_by_ready"], 1)
                    wait(v, "slots_by_ready", n - 3)
                    wait_scatter(v, k, turn, 6)
                    with nc.allow_low_precision(reason="whole numbers below 2**24, exact"):
                        v.tensor_reduce(slot[:, k % 2, :], slots_by[:].rearrange("p i c e -> p (i c) e"),
                                        AX.X, ALU.add).then_inc(s["slot_ready"], 1)

            def maxima(u, i):
                wait(v, f"scores{i}", u + 1)
                v.tensor_reduce(nmax[:, i, :], (S0, S1)[i][:].rearrange("p (h t) -> p h t", h=HEADS),
                                AX.X, ALU.max, negate=True).then_inc(s[f"max{i}"], 1)

            def reciprocals(u, i):
                wait(v, f"exp{i}", u + 1)
                wait(v, f"norm{i}", u)
                v.reciprocal(rsum[:, i, :], psum_p[:, i, :]).then_inc(s[f"rs{i}"], 1)

            def route(u, b):
                wait(v, "eg_ready", u + 1)
                wait(v, "sel_ready", u)
                v.tensor_scalar(egate1[:], egate[:], 1.0, None, ALU.add).then_inc(s["eg1_ready"], 1)
                wait(v, "eg1_ready", u + 1)
                wait(v, "topi_ready", u)
                v.reciprocal(gate[:], egate1[:]).then_inc(s["sel_ready"], 1)
                wait_apart(v, ("sel_ready", u + 1))
                for i in range(2):
                    ins = v.max(top[:, i, :], gate[:, i, :])
                ins.then_inc(s["top_ready"], 1)
                wait(v, "top_ready", u + 1)
                v.tensor_copy(xrow[:, b, :, :, GATE].rearrange("p c i -> p i c"), top[:, :, 0:2])\
                 .then_inc(s["gate_kept"], 1)
                wait_apart(v, ("topf_ready", u))
                for i in range(2):
                    ins = v.max_index(topi[:, i, :], top[:, i, :], gate[:, i, :])
                ins.then_inc(s["topi_ready"], 1)

            count = [0]

            def link(ins):
                count[0] += 1
                ins.then_inc(s["disp"], 1)
                v.wait_ge(s["disp"], count[0])

            def dispatch(h):
                v.wait_ge(s["carry_ready"], UNITS - 4 * (1 - h))
                v.tensor_copy(ends[:, h, :], carry[:, h, :]).then_inc(s["ends_ready"], 1)
                link(v.tensor_tensor(blocksi[:, 0, :], carry[:, h, :], round_up[:], ALU.add))
                link(v.tensor_scalar(blocksi[:, 1, :], blocksi[:, 0, :], 7, None, ALU.logical_shift_right))
                link(v.tensor_copy(blocksf[:], blocksi[:, 1, :]))
                link(v.tensor_tensor_scan(cum[:], ones_f[:], blocksf[:], 0.0, ALU.mult, ALU.add))
                link(v.tensor_scalar(below[:], cum[:], pidxf[:, 0:1], None, ALU.is_le))
                v.tensor_tensor(owned[:], below[:], blocksf[:], ALU.mult).then_inc(s["owned_ready"], 1)
                link(v.tensor_reduce(owner[:], below[:], AX.X, ALU.add))
                v.wait_ge(s["owned_ready"], h + 1)
                v.tensor_scalar(tab[:, 0, h:h + 1], owner[:], float(EXPERTS - 1), None, ALU.min)\
                 .then_inc(s["tab_ready"], 1)
                v.tensor_scalar(in_spares[:], owner[:], float(EXPERTS), spare[:, 0:1],
                                ALU.is_equal, ALU.mult)
                link(v.tensor_reduce(first[:], owned[:], AX.X, ALU.add))
                link(v.tensor_scalar(start[:], first[:], pidxf[:, 0:1], float(-P), ALU.subtract, ALU.mult))
                link(v.scalar_tensor_tensor(start[:], owner[:], float(CAP), start[:], ALU.mult, ALU.add))
                v.scalar_tensor_tensor(tab[:, 1, h:h + 1], start[:], float(EXPERTS * CAP), in_spares[:],
                                       ALU.min, ALU.add).then_inc(s["tab_ready"], 1)

            pipeline(v, step, after={-1: split_weights, 0: dispatch_tables, UNITS - 1: lambda: dispatch(0)})
            dispatch(1)


            def w(name, count):
                if not (isinstance(count, int) and count <= 0):
                    v.wait_ge(s_e[name], count)

            def expert_step(j, k):
                n = j * NX + k

                if is_block(n):
                    v.wait_ge(xg_in[k], 16 * (j + 1))
                    if not (isinstance(j, int) and j == 0):
                        v.wait_ge(yb_out[k % NY], 16 * (j * (NX // NY) - (1 if k < NY else 0)))
                    v.tensor_copy(meta[:, k, :], xg[:, k, DEST:GATE + 1])
                    v.tensor_copy(dest[:, k:k + 1], xg[:, k, DEST:GATE]).then_inc(s_e["meta_ready"], 1)
                if is_block(n - 1):
                    q = (k - 1) % 2
                    w("hid_done", n)
                    w("y_done", n - 2)
                    v.tensor_scalar(hid[:, q, :], (bank[2], bank[3])[q][:, 0:P], 0.0, None, ALU.max)\
                     .then_inc(s_e["hid_ready"], 1)
                if is_block(n - 2):
                    b, q = (k - 2) % NX, k % 2
                    w("y_done", n - 1)
                    sent = j * (NX // NY) + (k - 2) // NY
                    if not (isinstance(sent, int) and sent <= 0):
                        v.wait_ge(yb_out[b % NY], 16 * sent)
                    v.tensor_scalar(yb[:, b % NY, :], (bank[6], bank[7])[q][:, 0:D],
                                    meta[:, b, 1:2], None, ALU.mult).then_inc(s_e["y_copied"], 1)

            def add_choices(order, buf, use):
                v.wait_ge(ga_in[buf], 16 * (use + 1))
                if not (isinstance(use, int) and use == 0):
                    v.wait_ge(yo_out[buf], 16 * use)
                v.tensor_tensor(yo[:, buf], ga[:, buf, :, 0, :], ga[:, buf, :, 1, :], ALU.add)\
                 .then_inc(s_e["both_sum"], 1)

            def add_residual(order, unit, buf):
                v.wait_ge(s_e["both_sum"], order + 1)
                v.tensor_tensor(yo[:, buf], yo[:, buf], x_all[:, bass.ds(2 * unit, 2), :], ALU.add)\
                 .then_inc(s_e["y_ready"], 1)

            def combine_first(j, quarter):
                i, order = quarter // 2, (j - COMBINE) * 2 + quarter // 2
                if quarter % 2 == 0:
                    add_choices(order, i, j - COMBINE)
                else:
                    add_residual(order, first_half(j, i), i)

            experts(v, expert_step, combine_first)

            def combine_second(j):
                for k in range(NG):
                    order = UNITS // 2 + j * NG + k
                    add_choices(order, k, j + (UNITS // 4 if k < 2 else 0))
                    add_residual(order, second_half(j, k), k)

            combine_second(0)
            with v.Fori(1, UNITS // 8 - 1) as j:
                combine_second(j)
            combine_second(UNITS // 8 - 1)

        @block.gpsimd
        def _(pool):
            g = nc.gpsimd

            def clear():
                for t in (kbd, qz_h, qz_l):
                    g.memset(t[:].bitcast(F32), 0.0)
                g.memset(vbd[:], 0.0)
                g.iota(pidx[:], pattern=[[1, 1]], base=0, channel_multiplier=1).then_inc(s["init_pool"], 1)
                pool.wait_ge(s["consts_in"], 16 * CONSTS)

            def places():
                g.memset(expert_of[:], 0)
                pool.wait_ge(s["init_pool"], 1)
                g.tensor_copy(pidxf[:], pidx[:]).then_inc(s["disp_pool"], 1)
                g.iota(place[:, 0:16], pattern=[[4 * P, 4], [1, 2], [2 * P, 2]], base=0,
                       channel_multiplier=2)
                g.iota(place[:, 16:16 + SPARES], pattern=[[P, SPARES]], base=2 * TOKENS,
                       channel_multiplier=1)
                g.iota(place[:, 16 + SPARES:], pattern=[[1, TAILS]], base=2 * TOKENS + SPARES * P,
                       channel_multiplier=TAILS)
                g.memset(zrow[:], 0.0).then_inc(s["disp_pool"], 1)
                pool.wait_ge(s["disp_pool"], 2)
                g.tensor_copy(xrow[:, :, :, :, DEST],
                              place[:, 0:16].rearrange("p (b c i) -> p b c i", b=4, c=2))
                g.tensor_copy(zrow[:, 0:SPARES, DEST], place[:, 16:16 + SPARES])\
                 .then_inc(s["zrow_ready"], 1)
                pool.wait_ge(s["zrow_ready"], 1)
                for h in range(HALVES):
                    pool.dma_start(rows_in[h][EXPERTS * CAP:, :].rearrange("(b p) d -> p b d", p=P),
                                   zrow[:, 0:SPARES, :]).then_inc(s["spares_out"], 16)

            def tail_places():
                pool.wait_ge(s["spares_out"], 16 * HALVES)
                g.tensor_copy(zrow[:, :, DEST], place[:, 16 + SPARES:]).then_inc(s["zrow_ready"], 1)

            def deviations(n):
                a, b = live(n + 1), live(n - 3)
                if not (a or b):
                    return
                lo, hi = (0 if a else 2), (4 if b else 2)
                wait(pool, "ve_ready", n + 2)
                wait_last(pool, "xn_ready", n + 1)
                wait(pool, "xn2_ready", n - 3)
                wait_last(pool, "topi_ready", n - 4)
                g.tensor_tensor(rstd[:, lo:hi], ve[:, lo:hi], minus_half[:, lo:hi], ALU.pow)\
                 .then_inc(s["rstd_ready"], 1)

            def step(n, k, turn):
                if live(n - 4):
                    next_places(k, turn)
                if live(n):
                    u = n
                    others2 = others[:, None, :].broadcast_to([P, 2, SQ])
                    wait_apart(pool, ("adj_ready", u))
                    g.tensor_copy(adj_f[:], adj_sb[:, bass.ds(2 * u, 2), :]).then_inc(s["adj_cast"], 1)
                    wait(pool, "adj_cast", u + 1)
                    g.tensor_tensor(adj_f[:], adj_f[:], others2, ALU.mult).then_inc(s["adj_part"], 1)
                    wait(pool, "adj_part", u + 1)
                    wait(pool, "scores1", u)
                    g.tensor_tensor(adj_bias[:], others2, adj_f[:], ALU.subtract)\
                     .then_inc(s["adj_ready"], 1)
                deviations(n)
                if live(n - 5):
                    scatter(n - 5, k, turn, 0)
                if live(n - 1):
                    normalise_probs(n - 1, 0)
                if live(n - 4):
                    picks_of(n - 4)
                if live(n - 1):
                    normalise_probs(n - 1, 1)
                if live(n - 5):
                    scatter(n - 5, k, turn, 1)

            def next_places(k, turn):
                b, count = scattered(k, turn, 4)
                if isinstance(count, int):
                    if count <= 64:
                        return
                    gone = count - 64
                else:
                    gone = pool.to_reg(count - 64)
                pool.wait_ge(s["init_dve"], 2)
                pool.wait_ge(sc_out[b], gone)
                g.tensor_scalar(xrow[:, b, :, :, DEST], xrow[:, b, :, :, DEST], float(16 * P), None,
                                ALU.add)

            def scatter(u, k, turn, i):
                b, _ = scattered(k, turn, 5)
                copied = 16 * ((k - 5) // 4 + turn + 1)
                if not isinstance(copied, int):
                    copied = pool.to_reg(copied)
                wait_apart(pool, ("slot_ready", u + 1), ("gate_kept", u + 1))
                pool.wait_ge(row_copy[b], copied)
                for c in range(2):
                    at = slot[:, (k - 5) % 2, 2 * i + c:2 * i + c + 1]
                    pool.indirect_dma_start(
                        rows_in[half_of(u, b)], bass.IndirectOffsetOnAxis(ap=at, axis=0),
                        xrow[:, b, c, i, :], None).then_inc(sc_out[b], 16)

            def normalise_probs(u, i):
                wait(pool, f"rs{i}", u + 1)
                pr = probs[:, i, :].rearrange("p (h t) -> p h t", h=HEADS)
                g.tensor_tensor(pr, pr, rsum[:, i, :, None].broadcast_to([P, HEADS, SQ]), ALU.mult)\
                 .then_inc(s[f"norm{i}"], 1)

            def picks_of(u):
                wait_apart(pool, ("topi_ready", u + 1))
                g.tensor_copy(topf[:], topi[:, :, 0:2]).then_inc(s["topf_ready"], 1)
                wait_apart(pool, ("topf_ready", u + 1), ("ch_ready", u), ("slots_by_ready", u))
                for i in range(2):
                    for c in range(2):
                        ins = g.tensor_scalar(picks[:, i, c, :], iota[:], topf[:, i, c:c + 1], None,
                                              ALU.is_equal)
                ins.then_inc(s["oh_ready"], 1)
                wait(pool, "oh_ready", u + 1)
                wait(pool, "rank_done", u)
                g.tensor_tensor(chosen[:], picks[:, :, 0, :], picks[:, :, 1, :], ALU.add)\
                 .then_inc(s["ch_ready"], 1)

            pipeline(pool, step, after={-1: clear, 0: places, 2: tail_places})

            def send(j, k):
                copied = pool.to_reg(j * NX + k + 1)
                pool.wait_ge(s["init_dve"], 2)
                pool.wait_ge(s_e["y_copied"], copied)
                pool.indirect_dma_start(
                    results, bass.IndirectOffsetOnAxis(ap=dest[:, k:k + 1], axis=0),
                    yb[:, k % NY, :], None).then_inc(yb_out[k % NY], 16)

            with pool.Fori(0, BLOCKS // NX) as j:
                for k in range(NX):
                    send(j, k)


def kernel(**inputs):
    import numpy as np
    import concourse.bacc as bacc
    from concourse.bass_utils import run_bass_kernel_spmd

    def chunks(a):
        return np.ascontiguousarray(a.reshape(FC, P, -1).transpose(1, 0, 2))

    a = {k: np.asarray(v) for k, v in inputs.items()}
    arrays = {
        "x": a["x"],
        "adj": a["adj"],
        "wqkv": chunks(np.concatenate([a["L0_gnn_Wq"].T, a["L0_gnn_Wk"].T, a["L0_gnn_Wv"].T], axis=1)),
        "wo": chunks(a["L0_gnn_Wo"].T),
        "bqkv": np.ascontiguousarray(np.stack([a["L0_gnn_bq"], a["L0_gnn_bk"], a["L0_gnn_bv"]])
                                     .reshape(3, FC, P).transpose(2, 0, 1)),
        "bo": a["L0_gnn_bo"],
        "sel": chunks(a["L0_ffn_expert_sel"].T),
        "keys": np.ascontiguousarray(a["L0_ffn_keys"].reshape(EXPERTS, FC, P, HID).transpose(2, 0, 1, 3)),
        "values": np.ascontiguousarray(a["L0_ffn_values"].transpose(1, 0, 2)),
        **constants(),
    }
    nc = bacc.Bacc("TRN2", target_bir_lowering=False, num_devices=1)
    args = {k: nc.dram_tensor(f"in_{k}", v.shape, mybir.dt.from_np(v.dtype), kind="ExternalInput").ap()
            for k, v in arrays.items()}
    out = nc.dram_tensor("out_y", (BOARDS, SQ, D), F32, kind="ExternalOutput").ap()
    build(nc, out=out, **args)
    r = run_bass_kernel_spmd(nc, [{f"in_{k}": v for k, v in arrays.items()}], core_ids=[0])
    return r.results[0]["out_y"]
```
